# Optimizing a Trainium2 kernel written in Bass

```python
import numpy as np
import jax
import jax.numpy as jnp

def _softmax(x, axis=-1):
    return jax.nn.softmax(x, axis=axis)

def _gelu(x):
    return jax.nn.gelu(x, approximate=True)

def _silu(x):
    return jax.nn.silu(x)

def _sigmoid(x):
    return jax.nn.sigmoid(x)

def _layernorm(x, axis=-1, eps=1e-05):
    m = jnp.mean(x, axis=axis, keepdims=True)
    v = jnp.var(x, axis=axis, keepdims=True)
    return (x - m) / jnp.sqrt(v + eps)

def _scatter_add(tgt, idx, src, axis=0):
    return tgt.at[idx].add(src)

def _segment_sum(src, seg, n):
    return jax.ops.segment_sum(src, seg, n)
kernel_name = 'mk_macaron_d1_jaxref_r8_2fffa6'

def setup_inputs(seed: int=0):
    np.random.seed(seed)
    _w = jnp.asarray

    def _L0_attn_setup():
        import jax, jax.numpy as jnp
        import numpy as np
        H = 32
        KV = 8
        D = 128
        WINDOW = 128
        THETA = 10000.0

        def _rope_tables(seq_len, dtype=jnp.float32):
            inv_freq = 1.0 / THETA ** (jnp.arange(0, D, 2, dtype=jnp.float32) / D)
            t = jnp.arange(seq_len, dtype=jnp.float32)
            freqs = t[:, None] * inv_freq[None, :]
            emb = jnp.concatenate([freqs, freqs], axis=-1)
            return (jnp.cos(emb).astype(dtype), jnp.sin(emb).astype(dtype))

        def _rotate_half(x):
            x1, x2 = (x[..., :D // 2], x[..., D // 2:])
            return jnp.concatenate([-x2, x1], axis=-1)
        key = jax.random.key(seed)
        ks = jax.random.split(key, 5)
        B, S, E = (1, 256, 512)
        sc = 0.02
        return {'hidden_states': jax.random.normal(ks[0], (B, S, E), jnp.float32), 'Wq': jax.random.normal(ks[1], (H * D, E), jnp.float32) * sc, 'Wk': jax.random.normal(ks[2], (KV * D, E), jnp.float32) * sc, 'Wv': jax.random.normal(ks[3], (KV * D, E), jnp.float32) * sc, 'Wo': jax.random.normal(ks[4], (E, H * D), jnp.float32) * sc}
    _L0_attn_in = _L0_attn_setup()

    def _L0_ffn_setup():
        import jax, jax.numpy as jnp
        import numpy as np
        DIM = 512
        INTER = 128
        E = 16
        GROUPS = 4
        LIM = 2
        K = 2
        SHARED_INTER = 2 * INTER
        SCALE = 1.0
        key = jax.random.key(seed)
        ks = jax.random.split(key, 16)

        def n(k, shape, s=0.02):
            return jax.random.normal(k, shape, jnp.float32) * s
        return {'x': jax.random.normal(ks[0], (1, 256, DIM), jnp.float32), 'router_w': n(ks[1], (DIM, E)), 'router_b': n(ks[2], (E,)), 'router_bias': n(ks[3], (E,), 1.0), 'ew1': n(ks[4], (E, DIM, INTER)), 'eb1': n(ks[5], (E, INTER)), 'ew2': n(ks[6], (E, DIM, INTER)), 'eb2': n(ks[7], (E, INTER)), 'ew3': n(ks[8], (E, INTER, DIM)), 'eb3': n(ks[9], (E, DIM)), 'sw1': n(ks[10], (DIM, SHARED_INTER)), 'sb1': n(ks[11], (SHARED_INTER,)), 'sw2': n(ks[12], (DIM, SHARED_INTER)), 'sb2': n(ks[13], (SHARED_INTER,)), 'sw3': n(ks[14], (SHARED_INTER, DIM)), 'sb3': n(ks[15], (DIM,))}
    _L0_ffn_in = _L0_ffn_setup()
    _d = {'L0_attn_hidden_states': _L0_attn_in['hidden_states'], 'L0_attn_Wq': _L0_attn_in['Wq'], 'L0_attn_Wk': _L0_attn_in['Wk'], 'L0_attn_Wv': _L0_attn_in['Wv'], 'L0_attn_Wo': _L0_attn_in['Wo'], 'L0_ffn_router_w': _L0_ffn_in['router_w'], 'L0_ffn_router_b': _L0_ffn_in['router_b'], 'L0_ffn_router_bias': _L0_ffn_in['router_bias'], 'L0_ffn_ew1': _L0_ffn_in['ew1'], 'L0_ffn_eb1': _L0_ffn_in['eb1'], 'L0_ffn_ew2': _L0_ffn_in['ew2'], 'L0_ffn_eb2': _L0_ffn_in['eb2'], 'L0_ffn_ew3': _L0_ffn_in['ew3'], 'L0_ffn_eb3': _L0_ffn_in['eb3'], 'L0_ffn_sw1': _L0_ffn_in['sw1'], 'L0_ffn_sb1': _L0_ffn_in['sb1'], 'L0_ffn_sw2': _L0_ffn_in['sw2'], 'L0_ffn_sb2': _L0_ffn_in['sb2'], 'L0_ffn_sw3': _L0_ffn_in['sw3'], 'L0_ffn_sb3': _L0_ffn_in['sb3']}
    _x0 = _d['L0_attn_hidden_states']
    _d['L0_attn_hidden_states'] = jax.random.normal(jax.random.fold_in(jax.random.key(seed), 1), (8, 256, 512), dtype=_x0.dtype)
    del _x0
    return _d

def reference(L0_attn_hidden_states, L0_attn_Wq, L0_attn_Wk, L0_attn_Wv, L0_attn_Wo, L0_ffn_router_w, L0_ffn_router_b, L0_ffn_router_bias, L0_ffn_ew1, L0_ffn_eb1, L0_ffn_ew2, L0_ffn_eb2, L0_ffn_ew3, L0_ffn_eb3, L0_ffn_sw1, L0_ffn_sb1, L0_ffn_sw2, L0_ffn_sb2, L0_ffn_sw3, L0_ffn_sb3):

    def _L0_attn_ref(hidden_states, Wq, Wk, Wv, Wo):
        import jax, jax.numpy as jnp
        import numpy as np
        H = 32
        KV = 8
        D = 128
        WINDOW = 128
        THETA = 10000.0

        def _rope_tables(seq_len, dtype=jnp.float32):
            inv_freq = 1.0 / THETA ** (jnp.arange(0, D, 2, dtype=jnp.float32) / D)
            t = jnp.arange(seq_len, dtype=jnp.float32)
            freqs = t[:, None] * inv_freq[None, :]
            emb = jnp.concatenate([freqs, freqs], axis=-1)
            return (jnp.cos(emb).astype(dtype), jnp.sin(emb).astype(dtype))

        def _rotate_half(x):
            x1, x2 = (x[..., :D // 2], x[..., D // 2:])
            return jnp.concatenate([-x2, x1], axis=-1)
        B, S, E = hidden_states.shape
        q = (hidden_states @ Wq.T).reshape(B, S, H, D).transpose(0, 2, 1, 3)
        k = (hidden_states @ Wk.T).reshape(B, S, KV, D).transpose(0, 2, 1, 3)
        v = (hidden_states @ Wv.T).reshape(B, S, KV, D).transpose(0, 2, 1, 3)
        cos, sin = _rope_tables(S, hidden_states.dtype)
        cos = cos[None, None]
        sin = sin[None, None]
        q = q * cos + _rotate_half(q) * sin
        k = k * cos + _rotate_half(k) * sin
        k = jnp.repeat(k, H // KV, axis=1)
        v = jnp.repeat(v, H // KV, axis=1)
        scores = jnp.einsum('bhqd,bhkd->bhqk', q, k) / jnp.sqrt(jnp.asarray(D, q.dtype))
        i = jnp.arange(S)[:, None]
        j = jnp.arange(S)[None, :]
        band = jnp.abs(i - j) < WINDOW
        scores = jnp.where(band[None, None], -jnp.inf, scores)
        attn = jax.nn.softmax(scores, axis=-1)
        out = jnp.einsum('bhqk,bhkd->bhqd', attn, v)
        out = out.transpose(0, 2, 1, 3).reshape(B, S, H * D)
        return out @ Wo.T

    def _L0_ffn_ref(x, router_w, router_b, router_bias, ew1, eb1, ew2, eb2, ew3, eb3, sw1, sb1, sw2, sb2, sw3, sb3):
        import jax, jax.numpy as jnp
        import numpy as np
        DIM = 512
        INTER = 128
        E = 16
        GROUPS = 4
        LIM = 2
        K = 2
        SHARED_INTER = 2 * INTER
        SCALE = 1.0
        shape = x.shape
        xt = x.reshape(-1, DIM)
        T = xt.shape[0]
        logits = xt @ router_w + router_b
        scores = jax.nn.softmax(logits.astype(jnp.float32), axis=-1) + router_bias
        g = scores.reshape(T, GROUPS, E // GROUPS)
        _, gidx = jax.lax.top_k(g.max(axis=-1), LIM)
        keep = jnp.zeros((T, GROUPS), bool).at[jnp.arange(T)[:, None], gidx].set(True)
        masked = jnp.where(keep[:, :, None], g, -jnp.inf).reshape(T, E)
        _, idx = jax.lax.top_k(masked, K)
        vals = (jnp.take_along_axis(scores, idx, axis=1) * SCALE).astype(x.dtype)
        gate = jnp.zeros((T, E), x.dtype).at[jnp.arange(T)[:, None], idx].add(vals)

        def step(y, p):
            w1, b1, w2, b2, w3, b3, ge = p
            h = jax.nn.silu(xt @ w1 + b1) * (xt @ w2 + b2)
            return (y + ge[:, None] * (h @ w3 + b3), None)
        y, _ = jax.lax.scan(step, jnp.zeros_like(xt), (ew1, eb1, ew2, eb2, ew3, eb3, gate.T))
        z = jax.nn.silu(xt @ sw1 + sb1) * (xt @ sw2 + sb2) @ sw3 + sb3
        return (y + z).reshape(shape)
    x = L0_attn_hidden_states
    x = x + 0.5 * _L0_ffn_ref(_layernorm(x, axis=-1), L0_ffn_router_w, L0_ffn_router_b, L0_ffn_router_bias, L0_ffn_ew1, L0_ffn_eb1, L0_ffn_ew2, L0_ffn_eb2, L0_ffn_ew3, L0_ffn_eb3, L0_ffn_sw1, L0_ffn_sb1, L0_ffn_sw2, L0_ffn_sb2, L0_ffn_sw3, L0_ffn_sb3)
    x = x + _L0_attn_ref(_layernorm(x, axis=-1), L0_attn_Wq, L0_attn_Wk, L0_attn_Wv, L0_attn_Wo)
    x = x + 0.5 * _L0_ffn_ref(_layernorm(x, axis=-1), L0_ffn_router_w, L0_ffn_router_b, L0_ffn_router_bias, L0_ffn_ew1, L0_ffn_eb1, L0_ffn_ew2, L0_ffn_eb2, L0_ffn_ew3, L0_ffn_eb3, L0_ffn_sw1, L0_ffn_sb1, L0_ffn_sw2, L0_ffn_sb2, L0_ffn_sw3, L0_ffn_sb3)
    return x

_drawn_inputs = setup_inputs


def setup_inputs(seed=0):
    import zlib

    import numpy as np

    out = dict(_drawn_inputs(seed))
    spreads = {}
    factors = {'L0_ffn_router_w': 8.0,
     'L0_ffn_router_b': 192.708,
     'L0_ffn_eb1': 8.0,
     'L0_ffn_eb2': 8.0,
     'L0_ffn_sb1': 33.822,
     'L0_ffn_sb2': 32.89,
     'L0_ffn_sb3': 2.787}
    for name, (base, spread) in spreads.items():
        noise = np.random.default_rng([zlib.crc32(name.encode()), seed]).standard_normal(out[name].shape)
        drawn = base * np.exp(spread * noise) if base else spread * noise
        out[name] = jnp.asarray(drawn.astype(out[name].dtype))
    for name, factor in factors.items():
        out[name] = (out[name] * factor).astype(out[name].dtype)
    return out
```

```python
from contextlib import ExitStack

import concourse.bass as bass
from concourse import mybir

F32 = mybir.dt.float32
F32R = mybir.dt.float32r
ACT = mybir.ActivationFunctionType
ALU = mybir.AluOpType
AX_X = mybir.AxisListType.X

P = 128
BATCH, SEQ, DIM = 8, 256, 512
TOKENS = BATCH * SEQ
TILES = TOKENS // P
KT = DIM // P
CHUNK = 512
CHUNKS = TOKENS // CHUNK
CT = CHUNK // P

EXPERTS, INTER, GROUPS_R = 16, 128, 4
SLICES = EXPERTS + 2
SPG = 2
FGROUPS = SLICES // SPG
W_UP, W_DOWN = KT * INTER, DIM
W_SLICE = 2 * W_UP + W_DOWN
RAW_SLICE = W_SLICE + 2

HEADS, KV, HD = 32, 8, 128
QPK = HEADS // KV
W_QKV = (QPK + 2) * DIM
W_O = QPK * DIM
EPS = 1e-5
BIG = 1e30
PARTS = ((0, 0), (0, 1), (1, 0))


def bc(ap, shape):
    return ap.unsqueeze(len(shape) - 1).to_broadcast(list(shape))


def each(eng, count, body):
    body(0)
    with eng.Fori(1, count) as i:
        body(i)


def normalise(nc, ctx, tag, X, XT, ident, work, loaded, router_w=None, logits=None):
    xn, xt = work
    stats = ctx.enter_context(nc.sbuf_tensor(f"stats{tag}", [P, TILES, 6], F32))
    mean_var = ctx.enter_context(nc.sbuf_tensor(f"mean_var{tag}", [P, TILES, 2], F32))
    std = ctx.enter_context(nc.sbuf_tensor(f"std{tag}", [P, TILES], F32))
    rstd = ctx.enter_context(nc.sbuf_tensor(f"rstd{tag}", [P, TILES], F32))
    eps = ctx.enter_context(nc.sbuf_tensor(f"eps{tag}", [P, 1], F32))

    def sem(name):
        return ctx.enter_context(nc.semaphore(f"{name}{tag}"))

    stats_done, aggr_done, std_done, rstd_done = sem("stats_done"), sem("aggr_done"), sem("std_done"), sem("rstd_done")
    xn_ready, turned, xt_ready, high_ready, low_ready = (
        sem("xn_ready"), sem("turned"), sem("xt_ready"), sem("high_ready"), sem("low_ready"))
    eps_set, routed = sem("eps_set"), sem("routed")

    with ExitStack() as inner:
        bank = [inner.enter_context(nc.psum_tensor(f"turn{i}{tag}", [P, KT, P], F32)) for i in range(2)]
        block = inner.enter_context(nc.Block())

        @block.vector
        def _(dve):
            dve.memset(eps[:], EPS).then_inc(eps_set, 1)
            for t in range(TILES):
                if loaded is not None:
                    dve.wait_ge(loaded, 16 * (t // CT + 1))
                dve.bn_stats(stats[:, t, :], X[:, t, :]).then_inc(stats_done, 1)
            for t in range(TILES):
                dve.wait_ge(stats_done, t + 1)
                dve.bn_aggr(mean_var[:, t, :], stats[:, t, :]).then_inc(aggr_done, 1)
            dve.wait_ge(std_done, 1)
            dve.reciprocal(rstd[:], std[:]).then_inc(rstd_done, 1)
            dve.wait_ge(rstd_done, 1)
            def two_tiles(pair):
                t = pair * 2
                for b in range(2):
                    dve.wait_ge(turned, t)
                    dve.tensor_scalar(xn[:, b, :], X[:, t + b, :], mean_var[:, t + b, 0:1], rstd[:, bass.ds(t + b, 1)],
                                      ALU.subtract, ALU.mult).then_inc(xn_ready, 1)
                for b in range(2):
                    dve.wait_ge(high_ready, t + b + 1)
                    dve.tensor_tensor(XT[1][:, :, bass.ds((t + b) * P, P)], xt[:, b, :].rearrange("p (k n) -> p k n", k=KT),
                                      XT[0][:, :, bass.ds((t + b) * P, P)].bitcast(F32), ALU.subtract).then_inc(low_ready, 1)
            each(dve, TILES // 2, two_tiles)

        @block.scalar
        def _(act):
            act.wait_ge(eps_set, 1)
            act.wait_ge(aggr_done, TILES)
            act.activation(std[:], mean_var[:, :, 1], ACT.Sqrt, bias=eps[:, 0:1]).then_inc(std_done, 1)
            def two_tiles(pair):
                t = pair * 2
                for b in range(2):
                    act.wait_ge(turned, t + b + 1)
                    act.wait_ge(low_ready, t)
                    if router_w is not None:
                        act.wait_ge(routed, t)
                    act.activation(xt[:, b, :], bank[b][:].rearrange("p k n -> p (k n)"), ACT.Copy).then_inc(xt_ready, 1)
            each(act, TILES // 2, two_tiles)

        @block.gpsimd
        def _(pool):
            def two_tiles(pair):
                t = pair * 2
                for b in range(2):
                    pool.wait_ge(xt_ready, t + b + 1)
                    pool.tensor_copy(XT[0][:, :, bass.ds((t + b) * P, P)],
                                     xt[:, b, :].rearrange("p (k n) -> p k n", k=KT)).then_inc(high_ready, 1)
            each(pool, TILES // 2, two_tiles)

        @block.tensor
        def _(pe):
            def two_tiles(pair):
                t = pair * 2
                for b in range(2):
                    pe.wait_ge(xn_ready, t + b + 1)
                    pe.wait_ge(xt_ready, t)
                    for k in range(KT):
                        last = pe.transpose(bank[b][:, k, :], xn[:, b, k * P:(k + 1) * P], ident[:])
                    last.then_inc(turned, 1)
                if router_w is not None:
                    for b in range(2):
                        pe.wait_ge(xt_ready, t + b + 1)
                        for k in range(KT):
                            last = pe.matmul(logits[:, bass.ds((t + b) * EXPERTS, EXPERTS)], xt[:, b, k * P:(k + 1) * P],
                                             router_w[:, k, :], start=(k == 0), stop=(k == KT - 1))
                        last.then_inc(routed, 1)
            each(pe, TILES // 2, two_tiles)


def route(nc, ctx, tag, tmp, logits, router_b, router_bias, index, ident, gates, gates_dram, b3, X):
    def sem(name):
        return ctx.enter_context(nc.semaphore(f"{name}{tag}"))

    step, shifted, exped = sem("step"), sem("shifted"), sem("exped")
    gates_ready, gates_turned, gates_copied, ones_set = (
        sem("gates_ready"), sem("gates_turned"), sem("gates_copied"), sem("ones_set"))
    bias_done, bias_added, gates_out = sem("bias_done"), sem("bias_added"), sem("gates_out")

    n = TILES * EXPERTS
    spots = [tmp[:, i * n:(i + 1) * n] for i in range(12)]
    three = "p (t e) -> p t e"
    lg, ex, sc, ms, one1, eq, cand = [s.rearrange(three, t=TILES) for s in spots[:7]]
    col = [spots[7][:, i * TILES:(i + 1) * TILES] for i in range(8)]
    m, total, inv, m1, low = col[:5]
    small = [spots[8 + i // 4][:, (i % 4) * 64:(i % 4) * 64 + TILES * GROUPS_R] for i in range(8)]
    gmax, geq, gcand, keep1, keep2, gleft, pen = [s.rearrange(three, t=TILES) for s in small[:7]]
    G3 = (P, TILES, GROUPS_R)
    E3 = (P, TILES, EXPERTS)

    with ExitStack() as inner:
        bank = [inner.enter_context(nc.psum_tensor(f"gt{i}{tag}", [P, CHUNK], F32)) for i in range(2)]
        block = inner.enter_context(nc.Block())

        @block.vector
        def _(dve):
            done = [0]

            def link(ins):
                done[0] += 1
                ins.then_inc(step, 1)
                dve.wait_ge(step, done[0])

            def first_max(values, marks, equal, candidate, idx, shape):
                link(dve.tensor_reduce(m1, values, AX_X, ALU.max))
                link(dve.tensor_tensor(equal, values, bc(m1, shape), ALU.is_equal))
                link(dve.tensor_tensor(candidate, equal, idx, ALU.mult))
                link(dve.tensor_reduce(low, candidate, AX_X, ALU.min))
                link(dve.tensor_tensor(marks, candidate, bc(low, shape), ALU.is_equal))

            idx_e = index[:, 0:EXPERTS].unsqueeze(1).to_broadcast(list(E3))
            idx_g = index[:, 0:GROUPS_R].unsqueeze(1).to_broadcast(list(G3))
            rb = router_b.unsqueeze(1).to_broadcast(list(E3))
            rbias = router_bias.unsqueeze(1).to_broadcast(list(E3))
            dve.memset(gates[0:EXPERTS + 1, :], 1.0).then_inc(ones_set, 1)
            link(dve.tensor_tensor(lg, logits[:].rearrange(three, t=TILES), rb, ALU.add))
            link(dve.tensor_reduce(m, lg, AX_X, ALU.max))
            dve.tensor_tensor(lg, lg, bc(m, E3), ALU.subtract).then_inc(shifted, 1)
            dve.wait_ge(exped, 1)
            link(dve.tensor_reduce(total, ex, AX_X, ALU.add))
            link(dve.reciprocal(inv, total))
            link(dve.tensor_tensor(sc, ex, bc(inv, E3), ALU.mult))
            link(dve.tensor_tensor(sc, sc, rbias, ALU.add))
            link(dve.tensor_reduce(gmax, sc.rearrange("p t (g e) -> p t g e", g=GROUPS_R), AX_X, ALU.max))
            first_max(gmax, keep1, geq, gcand, idx_g, G3)
            link(dve.scalar_tensor_tensor(gleft, keep1, -2 * BIG, gmax, ALU.mult, ALU.add))
            first_max(gleft, keep2, geq, gcand, idx_g, G3)
            link(dve.tensor_tensor(keep1, keep1, keep2, ALU.add))
            link(dve.tensor_scalar(pen, keep1, -1.0, BIG, ALU.add, ALU.mult))
            link(dve.tensor_tensor(ms.rearrange("p t (g e) -> p t g e", g=GROUPS_R), sc.rearrange("p t (g e) -> p t g e", g=GROUPS_R),
                                   bc(pen, (P, TILES, GROUPS_R, EXPERTS // GROUPS_R)), ALU.add))
            first_max(ms, one1, eq, cand, idx_e, E3)
            link(dve.scalar_tensor_tensor(ms, one1, -2 * BIG, ms, ALU.mult, ALU.add))
            first_max(ms, lg, eq, cand, idx_e, E3)
            link(dve.tensor_tensor(one1, one1, lg, ALU.add))
            dve.tensor_tensor(sc, sc, one1, ALU.mult).then_inc(gates_ready, 1)
            for c in range(CHUNKS):
                dve.wait_ge(gates_turned, c + 1)
                dve.wait_ge(ones_set, 1)
                dve.tensor_copy(gates[0:EXPERTS, c * CHUNK:(c + 1) * CHUNK], bank[c % 2][0:EXPERTS, :]).then_inc(gates_copied, 1)
            for t in range(TILES):
                dve.wait_ge(bias_done, t + 1)
                dve.scalar_tensor_tensor(X[:, t, :], bank[t % 2][:], 0.5, X[:, t, :], ALU.mult, ALU.add).then_inc(bias_added, 1)

        @block.scalar
        def _(act):
            act.wait_ge(shifted, 1)
            act.activation(ex, lg, ACT.Exp).then_inc(exped, 1)

        @block.tensor
        def _(pe):
            pe.wait_ge(gates_ready, 1)
            for c in range(CHUNKS):
                if c >= 2:
                    pe.wait_ge(gates_copied, c - 1)
                for i in range(CT):
                    last = pe.transpose(bank[c % 2][0:EXPERTS, i * P:(i + 1) * P], sc[:, c * CT + i, :], ident[:])
                last.then_inc(gates_turned, 1)
            for t in range(TILES):
                pe.wait_ge(gates_copied, CHUNKS)
                if t >= 2:
                    pe.wait_ge(bias_added, t - 1)
                pe.matmul(bank[t % 2][:], gates[0:EXPERTS + 1, t * P:(t + 1) * P], b3[0:EXPERTS + 1, :],
                          start=True, stop=True).then_inc(bias_done, 1)

        @block.sync
        def _(sp):
            sp.wait_ge(gates_copied, CHUNKS)
            sp.dma_start(gates_dram[0:EXPERTS + 1, :], gates[0:EXPERTS + 1, :]).then_inc(gates_out, 16)
            sp.dma_start(gates_dram[EXPERTS + 1:SLICES, :], gates[EXPERTS:EXPERTS + 1, :]).then_inc(gates_out, 16)
            sp.wait_ge(gates_out, 32)


def experts(nc, ctx, tag, X, XT, raw, W, biases, gate_rows, gates_dram, work, w_dram, out_dram):
    silu, prod, gated, high, low = work

    def sem(name):
        return ctx.enter_context(nc.semaphore(f"{name}{tag}"))

    raw_in, w_high, w_low = [sem("raw_in0_"), sem("raw_in1_")], sem("w_high"), sem("w_low")
    gate_in = [sem(f"gate_in{c}_") for c in range(CHUNKS)]
    up1_done, up2_done, down_done, y_done = sem("up1_done"), sem("up2_done"), sem("down_done"), sem("y_done")
    silu_done, prod_done, gated_done, high_done, low_done, y_added = (
        sem("silu_done"), sem("prod_done"), sem("gated_done"), sem("high_done"), sem("low_done"), sem("y_added"))
    stored = sem("stored")

    with ExitStack() as inner:
        up1 = [inner.enter_context(nc.psum_tensor(f"up1_{j}{tag}", [P, CHUNK], F32)) for j in range(2)]
        up2 = [inner.enter_context(nc.psum_tensor(f"up2_{j}{tag}", [P, CHUNK], F32)) for j in range(2)]
        y = [inner.enter_context(nc.psum_tensor(f"y{t}{tag}", [P, DIM], F32)) for t in range(CT)]
        block = inner.enter_context(nc.Block())

        def over_groups(eng, group):
            def two_groups(pair):
                group(pair * 2, 0, False)
                group(pair * 2 + 1, 1, False)
            each(eng, (FGROUPS - 1) // 2, two_groups)
            group(FGROUPS - 1, 0, True)

        @block.sync
        def _(sp):
            def load_gates(g, c):
                rows = gates_dram[bass.ds(g * SPG, SPG), c * CHUNK:(c + 1) * CHUNK]
                sp.dma_start(gate_rows[:, c, :, :], rows.partition_broadcast(P)).then_inc(gate_in[c], 16)

            for j in range(SPG):
                sp.dma_start(raw[:, j, :], w_dram[j]).then_inc(raw_in[j], 16)
            for c in range(CHUNKS):
                load_gates(0, c)
            with sp.Fori(1, FGROUPS) as g:
                for j in range(SPG):
                    sp.wait_ge(w_high, (g - 1) * SPG + j + 1)
                    sp.wait_ge(w_low, (g - 1) * SPG + j + 1)
                    sp.dma_start(raw[:, j, :], w_dram[g * SPG + j]).then_inc(raw_in[j], 16)
                for c in range(CHUNKS):
                    sp.wait_ge(gated_done, ((g - 1) * CHUNKS + c) * 2 + 2)
                    load_gates(g, c)
            if out_dram is not None:
                for c in range(CHUNKS):
                    sp.wait_ge(y_added, ((FGROUPS - 1) * CHUNKS + c + 1) * CT)
                    sp.dma_start(out_dram[:, c * CT:(c + 1) * CT, :], X[:, c * CT:(c + 1) * CT, :]).then_inc(stored, 16)
                sp.wait_ge(stored, 16 * CHUNKS)

        @block.tensor
        def _(pe):
            def up(n, c, j, par):
                pe.wait_ge(prod_done, 2 * n)
                for bank, at, done in ((up1[j], 0, up1_done), (up2[j], W_UP, up2_done)):
                    for k in range(KT):
                        for i, (a, b) in enumerate(PARTS):
                            last = pe.matmul(bank[:], W[a][:, par, j, at + k * P:at + (k + 1) * P],
                                             XT[b][:, k, bass.ds(c * CHUNK, CHUNK)],
                                             start=(k == 0 and i == 0), stop=(k == KT - 1 and i == 2))
                    last.then_inc(done, 1)

            def down(n, j, par):
                pe.wait_ge(low_done, 2 * n + j + 1)
                if j == 0:
                    pe.wait_ge(y_added, CT * n)
                for t in range(CT):
                    for i, (a, b) in enumerate(PARTS):
                        last = pe.matmul(y[t][:], (high, low)[a][:, j, t * P:(t + 1) * P], W[b][:, par, j, 2 * W_UP:W_SLICE],
                                         start=(j == 0 and i == 0), stop=(j == SPG - 1 and i == 2))
                    if j == SPG - 1:
                        last.then_inc(y_done, 1)
                if j == 0:
                    last.then_inc(down_done, 1)

            def group(g, par, last_group):
                pe.wait_ge(w_high, SPG * g + SPG)
                pe.wait_ge(w_low, SPG * g + SPG)
                n0 = g * CHUNKS
                up(n0, 0, 0, par)
                up(n0, 0, 1, par)
                down(n0, 0, par)
                with pe.Fori(1, CHUNKS) as c:
                    up(n0 + c, c, 0, par)
                    down(n0 + c - 1, 1, par)
                    up(n0 + c, c, 1, par)
                    down(n0 + c, 0, par)
                down(n0 + CHUNKS - 1, 1, par)

            over_groups(pe, group)

        def raw_ready(eng, g, j):
            eng.wait_ge(raw_in[j], 16 * (g + 1))
            if not (isinstance(g, int) and g < 2):
                eng.wait_ge(y_added, (g - 1) * (CHUNKS * CT))

        @block.scalar
        def _(act):
            def split(g, j, par):
                raw_ready(act, g, j)
                act.activation(W[0][:, par, j, :], raw[:, j, 0:W_SLICE], ACT.Copy)
                act.activation(biases[:, par, j, :], raw[:, j, W_SLICE:RAW_SLICE], ACT.Copy).then_inc(w_high, 1)

            def step(n, j, par):
                act.wait_ge(up1_done, 2 * n + j + 1)
                act.wait_ge(prod_done, 2 * n)
                act.activation(silu[:, j, :], up1[j][:], ACT.Silu, bias=biases[:, par, j, 0:1]).then_inc(silu_done, 1)
                act.wait_ge(gated_done, 2 * n + j + 1)
                if j == 0:
                    act.wait_ge(down_done, n)
                else:
                    act.wait_ge(y_done, CT * n)
                act.activation(high[:, j, :], gated[:, j, :], ACT.Copy).then_inc(high_done, 1)

            def group(g, par, last_group):
                n0 = g * CHUNKS
                for j in range(SPG):
                    act.wait_ge(w_high, SPG * g + SPG)
                    step(n0, j, par)
                    if not last_group:
                        split(g + 1, j, 1 - par)
                with act.Fori(1, CHUNKS) as c:
                    for j in range(SPG):
                        step(n0 + c, j, par)

            for j in range(SPG):
                split(0, j, 0)
            over_groups(act, group)

        @block.gpsimd
        def _(pool):
            def split(g, j, par):
                raw_ready(pool, g, j)
                pool.wait_ge(w_high, SPG * g + j + 1)
                pool.tensor_tensor(W[1][:, par, j, :], raw[:, j, 0:W_SLICE], W[0][:, par, j, :].bitcast(F32),
                                   ALU.subtract).then_inc(w_low, 1)

            def step(n, j):
                pool.wait_ge(high_done, 2 * n + j + 1)
                pool.tensor_tensor(low[:, j, :], gated[:, j, :], high[:, j, :].bitcast(F32), ALU.subtract).then_inc(low_done, 1)

            def group(g, par, last_group):
                n0 = g * CHUNKS
                for j in range(SPG):
                    step(n0, j)
                    if not last_group:
                        split(g + 1, j, 1 - par)
                with pool.Fori(1, CHUNKS) as c:
                    for j in range(SPG):
                        step(n0 + c, j)

            for j in range(SPG):
                split(0, j, 0)
            over_groups(pool, group)

        @block.vector
        def _(dve):
            def step(n, c, j, par, g):
                dve.wait_ge(up2_done, 2 * n + j + 1)
                dve.wait_ge(silu_done, 2 * n + j + 1)
                dve.scalar_tensor_tensor(prod[:, j, :], up2[j][:], biases[:, par, j, 1:2], silu[:, j, :],
                                         ALU.add, ALU.mult).then_inc(prod_done, 1)
                dve.wait_ge(prod_done, 2 * n + j + 1)
                dve.wait_ge(low_done, 2 * n)
                dve.tensor_tensor(gated[:, j, :], prod[:, j, :], gate_rows[:, c, j, :], ALU.mult).then_inc(gated_done, 1)

            def add(n, c):
                for t in range(CT):
                    dve.wait_ge(y_done, CT * n + t + 1)
                    dve.scalar_tensor_tensor(X[:, c * CT + t, :], y[t][:], 0.5, X[:, c * CT + t, :],
                                             ALU.mult, ALU.add).then_inc(y_added, 1)

            def group(g, par, last_group):
                n0 = g * CHUNKS
                for c in range(CHUNKS):
                    dve.wait_ge(gate_in[c], 16 * (g + 1))
                step(n0, 0, 0, par, g)
                step(n0, 0, 1, par, g)
                with dve.Fori(1, CHUNKS) as c:
                    step(n0 + c, c, 0, par, g)
                    add(n0 + c - 1, c - 1)
                    step(n0 + c, c, 1, par, g)
                add(n0 + CHUNKS - 1, CHUNKS - 1)

            over_groups(dve, group)


def attention(nc, ctx, X, XT, ident, a_dram, consts_dram):
    def sb(name, shape, dt=F32):
        return ctx.enter_context(nc.sbuf_tensor(name, shape, dt))

    def sem(name):
        return ctx.enter_context(nc.semaphore(name))

    raw_qkv, raw_o = sb("raw_qkv", [P, W_QKV]), sb("raw_o", [P, W_O])
    Wqkv = [sb("wqkv_high", [P, W_QKV], F32R), sb("wqkv_low", [P, W_QKV], F32R)]
    Wo = [sb("wo_high", [P, W_O], F32R), sb("wo_low", [P, W_O], F32R)]
    rotary = sb("rotary", [P, 2, SEQ])
    masks = sb("masks", [P, 2, P])
    swapped, straight = sb("swapped", [P, 2, CHUNK]), sb("straight", [P, 2, CHUNK])
    qk = sb("qk", [P, QPK + 1, CHUNK])
    v_turned, v = sb("v_turned", [P, CHUNK]), sb("v", [P, CT, HD])
    probs, probs_t = sb("probs", [P, 2, QPK, P]), sb("probs_t", [P, 2, QPK * P])
    row_max, row_sum, row_inv = sb("row_max", [P, 2, QPK]), sb("row_sum", [P, 2, QPK]), sb("row_inv", [P, 2, QPK])
    heads_out = [sb("heads_high", [P, QPK, CHUNK], F32R), sb("heads_low", [P, QPK, CHUNK], F32R)]

    names = ("consts_in raw_qkv_in raw_o_in qkv_high qkv_low o_high o_low proj_done swap_done rope_mul rope_sin rope_add "
             "vt_copied v_turned_back v_copied scored masked max_done sub_done exp_done sum_done inv_done p_ready "
             "p_turned pt_copied pv_done oh_done ol_done wo_done added").split()
    s = {name: sem("a_" + name) for name in names}
    (consts_in, raw_qkv_in, raw_o_in, qkv_high, qkv_low, o_high, o_low, proj_done, swap_done, rope_mul, rope_sin, rope_add,
     vt_copied, v_back, v_copied, scored, masked, max_done, sub_done, exp_done, sum_done, inv_done, p_ready,
     p_turned, pt_copied, pv_done, oh_done, ol_done, wo_done, added) = [s[x] for x in names]
    ROPES, PROJ = QPK + 1, QPK + 2
    NCH = KV * CHUNKS
    scale = float(HD) ** -0.5
    H = HD // 2

    with ExitStack() as inner:
        def bank(name, shape):
            return inner.enter_context(nc.psum_tensor(name, shape, F32))
        proj = [bank(f"proj{i}", [P, CHUNK]) for i in range(2)]
        score = [bank(f"score{i}", [P, QPK, P]) for i in range(2)]
        turn = bank("turn", [P, CT, P])
        pv = bank("pv", [P, QPK, P])
        yo = [bank(f"yo{i}", [P, DIM]) for i in range(2)]
        block = inner.enter_context(nc.Block())

        @block.sync
        def _(sp):
            sp.dma_start(raw_qkv[:], a_dram[0, :, 0:W_QKV]).then_inc(raw_qkv_in, 16)
            sp.dma_start(rotary[:], consts_dram[:, P:P + 2 * SEQ].rearrange("p (a b) -> p a b", a=2)).then_inc(consts_in, 16)
            sp.dma_start(masks[:], consts_dram[:, P + 2 * SEQ:2 * SEQ + 3 * P].rearrange("p (a b) -> p a b", a=2)).then_inc(consts_in, 16)
            sp.dma_start(raw_o[:], a_dram[0, :, W_QKV:W_QKV + W_O]).then_inc(raw_o_in, 16)
            with sp.Fori(1, KV) as g:
                sp.wait_ge(qkv_low, PROJ * g)
                sp.dma_start(raw_qkv[:], a_dram[g, :, 0:W_QKV]).then_inc(raw_qkv_in, 16)
                sp.wait_ge(o_low, QPK * g)
                sp.dma_start(raw_o[:], a_dram[g, :, W_QKV:W_QKV + W_O]).then_inc(raw_o_in, 16)

        @block.tensor
        def _(pe):
            def project(n, g, c, i):
                pe.wait_ge(qkv_low, PROJ * g + i + 1)
                if i == 1:
                    pe.wait_ge(vt_copied, n)
                else:
                    pe.wait_ge(rope_mul, ROPES * n + max(i - 1, 0))
                for k in range(KT):
                    for m, (a, b) in enumerate(PARTS):
                        last = pe.matmul(proj[i % 2][:], Wqkv[a][:, i * DIM + k * P:i * DIM + (k + 1) * P],
                                         XT[b][:, k, bass.ds(c * CHUNK, CHUNK)],
                                         start=(k == 0 and m == 0), stop=(k == KT - 1 and m == 2))
                last.then_inc(proj_done, 1)

            def out_proj(n, g, t):
                pe.wait_ge(o_low, QPK * g + QPK)
                pe.wait_ge(ol_done, CT * n + t + 1)
                pe.wait_ge(added, CT * n + max(t - 1, 0))
                for h in range(QPK):
                    for m, (a, b) in enumerate(PARTS):
                        last = pe.matmul(yo[t % 2][:], heads_out[a][:, h, t * P:(t + 1) * P], Wo[b][:, h * DIM:(h + 1) * DIM],
                                         start=(h == 0 and m == 0), stop=(h == QPK - 1 and m == 2))
                last.then_inc(wo_done, 1)

            def turn_v(n):
                pe.wait_ge(vt_copied, n + 1)
                pe.wait_ge(pt_copied, CT * n)
                for t in range(CT):
                    last = pe.transpose(turn[:, t, :], v_turned[:, t * P:(t + 1) * P], ident[:])
                last.then_inc(v_back, 1)

            def scores(n, u):
                pe.wait_ge(rope_add, ROPES * (n + 1))
                pe.wait_ge(masked, CT * n + max(u - 1, 0))
                key_tile = u ^ 1
                for h in range(QPK):
                    last = pe.matmul(score[u % 2][:, h, :], qk[:, 1 + h, u * P:(u + 1) * P],
                                     qk[:, 0, key_tile * P:(key_tile + 1) * P], start=True, stop=True)
                last.then_inc(scored, 1)

            def turn_probs(n, u):
                pe.wait_ge(p_ready, CT * n + u + 1)
                if u == 0:
                    pe.wait_ge(v_copied, n + 1)
                else:
                    pe.wait_ge(pt_copied, CT * n + u)
                for h in range(QPK):
                    last = pe.transpose(turn[:, h, :], probs[:, u % 2, h, :], ident[:])
                last.then_inc(p_turned, 1)

            def mix(n, u):
                pe.wait_ge(pt_copied, CT * n + u + 1)
                pe.wait_ge(ol_done, CT * n + u)
                pe.matmul(pv[:].rearrange("p h q -> p (h q)"), v[:, u ^ 1, :], probs_t[:, u % 2, :],
                          start=True, stop=True).then_inc(pv_done, 1)

            def chunk(n, g, c, before):
                for i in range(PROJ):
                    project(n, g, c, i)
                if before:
                    out_proj(*before, 0)
                turn_v(n)
                scores(n, 0)
                scores(n, 1)
                if before:
                    out_proj(*before, 1)
                    out_proj(*before, 2)
                turn_probs(n, 0)
                scores(n, 2)
                turn_probs(n, 1)
                scores(n, 3)
                mix(n, 0)
                mix(n, 1)
                if before:
                    out_proj(*before, 3)
                turn_probs(n, 2)
                mix(n, 2)
                turn_probs(n, 3)
                mix(n, 3)

            chunk(0, 0, 0, None)
            with pe.Fori(1, NCH) as n:
                chunk(n, n // CHUNKS, n % CHUNKS, (n - 1, (n - 1) // CHUNKS))
            for t in range(CT):
                out_proj(NCH - 1, KV - 1, t)

        def by_head(eng, body, split_qkv, split_o):
            for i in range(PROJ):
                split_qkv(0, i)

            def head(g, last):
                body(g * CHUNKS, lambda u: None)
                for h in range(QPK):
                    split_o(g, h)
                with eng.Fori(1, CHUNKS - 1) as c:
                    body(g * CHUNKS + c, lambda u: None)

                def after(u):
                    if not last and u < 3:
                        split_qkv(g + 1, 2 * u)
                        split_qkv(g + 1, 2 * u + 1)
                body(g * CHUNKS + CHUNKS - 1, after)

            each(eng, KV - 1, lambda g: head(g, False))
            head(KV - 1, True)

        @block.scalar
        def _(act):
            def split_qkv(g, i):
                act.wait_ge(raw_qkv_in, 16 * (g + 1))
                if not (isinstance(g, int) and g == 0):
                    act.wait_ge(proj_done, PROJ * CHUNKS * g - PROJ + i + 1)
                act.activation(Wqkv[0][:, i * DIM:(i + 1) * DIM], raw_qkv[:, i * DIM:(i + 1) * DIM], ACT.Copy).then_inc(qkv_high, 1)

            def split_o(g, h):
                act.wait_ge(raw_o_in, 16 * (g + 1))
                act.wait_ge(wo_done, CHUNKS * CT * g)
                act.activation(Wo[0][:, h * DIM:(h + 1) * DIM], raw_o[:, h * DIM:(h + 1) * DIM], ACT.Copy).then_inc(o_high, 1)

            def body(n, after):
                for r in range(ROPES):
                    act.wait_ge(proj_done, PROJ * n + r + 1)
                    act.wait_ge(rope_add, ROPES * n + max(r - 1, 0))
                    act.activation(swapped[0:H, r % 2, :], proj[r % 2][H:HD, :], ACT.Copy)
                    act.activation(swapped[H:HD, r % 2, :], proj[r % 2][0:H, :], ACT.Copy).then_inc(swap_done, 1)
                act.wait_ge(proj_done, PROJ * (n + 1))
                act.wait_ge(v_back, n)
                act.activation(v_turned[:], proj[1][:], ACT.Copy).then_inc(vt_copied, 1)
                act.wait_ge(v_back, n + 1)
                act.wait_ge(pv_done, CT * n)
                act.activation(v[:], turn[:], ACT.Copy).then_inc(v_copied, 1)

                def exp(u):
                    act.wait_ge(sub_done, CT * n + u + 1)
                    act.activation(probs[:, u % 2, :, :], probs[:, u % 2, :, :], ACT.Exp, scale=scale).then_inc(exp_done, 1)

                def copy_turned(u):
                    act.wait_ge(p_turned, CT * n + u + 1)
                    act.wait_ge(pv_done, CT * n + max(u - 1, 0))
                    act.activation(probs_t[:, u % 2, :], turn[:].rearrange("p h q -> p (h q)"), ACT.Copy).then_inc(pt_copied, 1)

                def high(u):
                    act.wait_ge(pv_done, CT * n + u + 1)
                    act.activation(heads_out[0][:, :, u * P:(u + 1) * P], pv[:], ACT.Copy).then_inc(oh_done, 1)

                exp(0)
                exp(1)
                copy_turned(0)
                copy_turned(1)
                high(0)
                after(0)
                exp(2)
                high(1)
                exp(3)
                copy_turned(2)
                after(1)
                high(2)
                copy_turned(3)
                after(2)
                high(3)

            by_head(act, body, split_qkv, split_o)

        @block.gpsimd
        def _(pool):
            def split_qkv(g, i):
                pool.wait_ge(qkv_high, PROJ * g + i + 1)
                cols = slice(i * DIM, (i + 1) * DIM)
                pool.tensor_tensor(Wqkv[1][:, cols], raw_qkv[:, cols], Wqkv[0][:, cols].bitcast(F32), ALU.subtract).then_inc(qkv_low, 1)

            def split_o(g, h):
                pool.wait_ge(o_high, QPK * g + h + 1)
                cols = slice(h * DIM, (h + 1) * DIM)
                pool.tensor_tensor(Wo[1][:, cols], raw_o[:, cols], Wo[0][:, cols].bitcast(F32), ALU.subtract).then_inc(o_low, 1)

            def body(n, after):
                for r in range(ROPES):
                    pool.wait_ge(swap_done, ROPES * n + r + 1)
                    part = swapped[:, r % 2, :].rearrange("p (b s) -> p b s", s=SEQ)
                    pool.tensor_tensor(part, part, rotary[:, 1, :].unsqueeze(1).to_broadcast([P, CHUNK // SEQ, SEQ]),
                                       ALU.mult).then_inc(rope_sin, 1)

                def subtract(u):
                    pool.wait_ge(max_done, CT * n + u + 1)
                    pool.tensor_tensor(probs[:, u % 2, :, :], probs[:, u % 2, :, :], bc(row_max[:, u % 2, :], (P, QPK, P)),
                                       ALU.subtract).then_inc(sub_done, 1)

                def divide(u):
                    pool.wait_ge(inv_done, CT * n + u + 1)
                    pool.tensor_tensor(probs[:, u % 2, :, :], probs[:, u % 2, :, :], bc(row_inv[:, u % 2, :], (P, QPK, P)),
                                       ALU.mult).then_inc(p_ready, 1)

                subtract(0)
                subtract(1)
                divide(0)
                divide(1)
                after(0)
                subtract(2)
                subtract(3)
                divide(2)
                after(1)
                divide(3)
                after(2)

            pool.wait_ge(consts_in, 32)
            by_head(pool, body, split_qkv, split_o)

        @block.vector
        def _(dve):
            def multiply(n, r):
                dve.wait_ge(swap_done, ROPES * n + r + 1)
                dve.wait_ge(rope_add, ROPES * n + max(r - 1, 0))
                dve.tensor_tensor(straight[:, r % 2, :].rearrange("p (b s) -> p b s", s=SEQ),
                                  proj[r % 2][:].rearrange("p (b s) -> p b s", s=SEQ),
                                  rotary[:, 0, :].unsqueeze(1).to_broadcast([P, CHUNK // SEQ, SEQ]), ALU.mult).then_inc(rope_mul, 1)

            def add_halves(n, r):
                dve.wait_ge(rope_sin, ROPES * n + r + 1)
                dve.wait_ge(rope_mul, ROPES * n + r + 1)
                dve.wait_ge(scored, CT * n)
                dve.tensor_tensor(qk[:, r, :], straight[:, r % 2, :], swapped[:, r % 2, :], ALU.add).then_inc(rope_add, 1)

            def mask_and_max(n, u):
                dve.wait_ge(scored, CT * n + u + 1)
                dve.wait_ge(p_turned, CT * n + max(u - 1, 0))
                dve.tensor_tensor(probs[:, u % 2, :, :], score[u % 2][:],
                                  masks[:, u % 2, :].unsqueeze(1).to_broadcast([P, QPK, P]), ALU.add).then_inc(masked, 1)
                dve.wait_ge(masked, CT * n + u + 1)
                dve.wait_ge(sub_done, CT * n + max(u - 1, 0))
                dve.tensor_reduce(row_max[:, u % 2, :], probs[:, u % 2, :, :], AX_X, ALU.max).then_inc(max_done, 1)

            def inverse_sum(n, u):
                dve.wait_ge(exp_done, CT * n + u + 1)
                dve.tensor_reduce(row_sum[:, u % 2, :], probs[:, u % 2, :, :], AX_X, ALU.add).then_inc(sum_done, 1)
                dve.wait_ge(sum_done, CT * n + u + 1)
                dve.wait_ge(p_ready, CT * n + max(u - 1, 0))
                dve.reciprocal(row_inv[:, u % 2, :], row_sum[:, u % 2, :]).then_inc(inv_done, 1)

            def low(n, u):
                dve.wait_ge(oh_done, CT * n + u + 1)
                dve.tensor_tensor(heads_out[1][:, :, u * P:(u + 1) * P], pv[:],
                                  heads_out[0][:, :, u * P:(u + 1) * P].bitcast(F32), ALU.subtract).then_inc(ol_done, 1)

            def add_out(n, c, t):
                dve.wait_ge(wo_done, CT * n + t + 1)
                dve.tensor_tensor(X[:, c * CT + t, :], yo[t % 2][:], X[:, c * CT + t, :], ALU.add).then_inc(added, 1)

            def chunk(n, before):
                for r in range(ROPES):
                    multiply(n, r)
                    if r:
                        add_halves(n, r - 1)
                add_halves(n, ROPES - 1)
                if before:
                    add_out(*before, 0)
                mask_and_max(n, 0)
                mask_and_max(n, 1)
                inverse_sum(n, 0)
                inverse_sum(n, 1)
                if before:
                    add_out(*before, 1)
                    add_out(*before, 2)
                mask_and_max(n, 2)
                mask_and_max(n, 3)
                low(n, 0)
                inverse_sum(n, 2)
                low(n, 1)
                inverse_sum(n, 3)
                if before:
                    add_out(*before, 3)
                low(n, 2)
                low(n, 3)

            dve.wait_ge(consts_in, 32)
            chunk(0, None)
            with dve.Fori(1, NCH) as n:
                chunk(n, (n - 1, (n - 1) % CHUNKS))
            for t in range(CT):
                add_out(NCH - 1, CHUNKS - 1, t)


def macaron_block(nc, x, w_ffn, b3_dram, router_dram, rows_dram, w_attn, consts_dram, out):
    x_v = x.rearrange("(t p) d -> p t d", p=P)
    out_v = out.rearrange("(t p) d -> p t d", p=P)
    gates_dram = nc.dram_tensor("gates_dram", [SLICES, TOKENS], F32, kind="Internal").ap()

    with ExitStack() as ctx:
        def sb(name, shape, dt=F32):
            return ctx.enter_context(nc.sbuf_tensor(name, shape, dt))
        X = sb("X", [P, TILES, DIM])
        XT = [sb("xt_high", [P, KT, TOKENS], F32R), sb("xt_low", [P, KT, TOKENS], F32R)]
        ident = sb("ident", [P, P])
        x_in, ident_in = ctx.enter_context(nc.semaphore("x_in")), ctx.enter_context(nc.semaphore("ident_in"))

        def ffn(tag, first, last):
            with ExitStack() as own:
                def sb(name, shape, dt=F32):
                    return own.enter_context(nc.sbuf_tensor(name + tag, shape, dt))
                raw = sb("raw", [P, SPG, RAW_SLICE])
                W = [sb("w_high_", [P, 2, SPG, W_SLICE], F32R), sb("w_low_", [P, 2, SPG, W_SLICE], F32R)]
                biases = sb("biases", [P, 2, SPG, 2])
                gate_rows = sb("gate_rows", [P, CHUNKS, SPG, CHUNK])
                silu, prod, gated = (sb(x, [P, 2, CHUNK]) for x in ("silu", "prod", "gated"))
                high, low = sb("h_high", [P, 2, CHUNK], F32R), sb("h_low", [P, 2, CHUNK], F32R)
                tmp = gate_rows[:].rearrange("p c j n -> p (c j n)")
                gates = raw[:].rearrange("p j n -> p (j n)")[:, 0:TOKENS]
                b3 = prod[:, 0, :]
                router_w = sb("router_w", [P, KT, EXPERTS])
                rows = sb("rows", [P, 3, EXPERTS])
                params_in = own.enter_context(nc.semaphore("params_in" + tag))
                with nc.psum_tensor("logits" + tag, [P, TILES * EXPERTS], F32) as logits:
                    with nc.Block() as block:
                        @block.sync
                        def _(sp):
                            if first:
                                for c in range(CHUNKS):
                                    sp.dma_start(X[:, c * CT:(c + 1) * CT, :], x_v[:, c * CT:(c + 1) * CT, :]).then_inc(x_in, 16)
                                sp.dma_start(ident[:], consts_dram[:, 0:P]).then_inc(ident_in, 16)
                                sp.wait_ge(x_in, 16 * CHUNKS)
                                sp.wait_ge(ident_in, 16)
                            sp.dma_start(router_w[:], router_dram).then_inc(params_in, 16)
                            sp.dma_start(rows[:], rows_dram.partition_broadcast(P)).then_inc(params_in, 16)
                            sp.dma_start(b3[0:EXPERTS + 1, :], b3_dram).then_inc(params_in, 16)
                            sp.wait_ge(params_in, 48)
                    normalise(nc, own, tag, X, XT, ident, (silu, gated), None, router_w, logits)
                    route(nc, own, tag, tmp, logits, rows[:, 0, :], rows[:, 1, :], rows[:, 2, :], ident, gates, gates_dram, b3, X)
                experts(nc, own, tag, X, XT, raw, W, biases, gate_rows, gates_dram,
                        (silu, prod, gated, high, low), w_ffn, out_v if last else None)

        ffn("_f1", True, False)
        with ExitStack() as own:
            turning = [own.enter_context(nc.sbuf_tensor(x, [P, 2, CHUNK], F32)) for x in ("a_xn", "a_xt")]
            normalise(nc, own, "_a", X, XT, ident, turning, None)
        with ExitStack() as own:
            attention(nc, own, X, XT, ident, w_attn, consts_dram)
        ffn("_f2", False, True)


def kernel(**inputs):
    import numpy as _np
    import concourse.bacc as _bacc
    from concourse import mybir as _mybir
    from concourse.bass_utils import run_bass_kernel_spmd as _run

    a = {k.replace("L0_", ""): _np.asarray(v) for k, v in inputs.items()}

    def up(w):
        return w.reshape(-1, KT, P, INTER).transpose(0, 2, 1, 3).reshape(-1, P, W_UP)

    def halves(w):
        return w.reshape(DIM, 2, INTER).transpose(1, 0, 2)

    def heads(w, n):
        return w.reshape(KV, n // KV, HD, KT, P).transpose(0, 4, 1, 3, 2).reshape(KV, P, -1)

    w1 = _np.concatenate([a["ffn_ew1"], halves(a["ffn_sw1"])])
    w2 = _np.concatenate([a["ffn_ew2"], halves(a["ffn_sw2"])])
    w3 = _np.concatenate([a["ffn_ew3"], a["ffn_sw3"].reshape(2, INTER, DIM)])
    b1 = _np.concatenate([a["ffn_eb1"], a["ffn_sb1"].reshape(2, INTER)])
    b2 = _np.concatenate([a["ffn_eb2"], a["ffn_sb2"].reshape(2, INTER)])
    w_ffn = _np.concatenate([up(w1), up(w2), w3, b1[:, :, None], b2[:, :, None]], axis=2)
    b3 = _np.concatenate([a["ffn_eb3"], a["ffn_sb3"][None]])
    router = a["ffn_router_w"].reshape(KT, P, EXPERTS).transpose(1, 0, 2)
    rows = _np.stack([a["ffn_router_b"], a["ffn_router_bias"], _np.arange(EXPERTS, dtype=_np.float32) - 64.0])
    w_o = a["attn_Wo"].reshape(DIM, KV, QPK, HD).transpose(1, 3, 2, 0).reshape(KV, P, W_O)
    w_attn = _np.concatenate([heads(a["attn_Wk"], KV), heads(a["attn_Wq"], HEADS), heads(a["attn_Wv"], KV), w_o], axis=2)

    inv_freq = (1.0 / _np.float32(10000.0) ** (_np.arange(0, HD, 2, dtype=_np.float32) / _np.float32(HD))).astype(_np.float32)
    freqs = _np.arange(SEQ, dtype=_np.float32)[None, :] * inv_freq[:, None]
    cos = _np.cos(_np.concatenate([freqs, freqs])).astype(_np.float32)
    sin = _np.concatenate([-_np.sin(freqs), _np.sin(freqs)]).astype(_np.float32)
    q, k = _np.arange(P)[:, None], _np.arange(P)[None, :]
    mask = _np.concatenate([_np.where(k >= q, 0.0, -BIG), _np.where(k <= q, 0.0, -BIG)], axis=1).astype(_np.float32)
    consts = _np.concatenate([_np.eye(P, dtype=_np.float32), cos, sin, mask], axis=1)

    arrays = {"x": a["attn_hidden_states"].reshape(TOKENS, DIM), "w_ffn": w_ffn, "b3": b3, "router": router,
              "rows": rows, "w_attn": w_attn, "consts": consts}
    nc = _bacc.Bacc("TRN2", target_bir_lowering=False, num_devices=1)
    args = []
    for name in arrays:
        arrays[name] = _np.ascontiguousarray(arrays[name])
        args.append(nc.dram_tensor(name, arrays[name].shape, _mybir.dt.from_np(arrays[name].dtype), kind="ExternalInput").ap())
    args.append(nc.dram_tensor("out", (TOKENS, DIM), _mybir.dt.float32, kind="ExternalOutput").ap())
    macaron_block(nc, *args)
    r = _run(nc, [arrays], core_ids=[0])
    return r.results[0]["out"].reshape(BATCH, SEQ, DIM)
```

```python
from contextlib import ExitStack

import concourse.bass as bass
from concourse import mybir

F32 = mybir.dt.float32
F32R = mybir.dt.float32r
ACT = mybir.ActivationFunctionType
ALU = mybir.AluOpType
AX_X = mybir.AxisListType.X

P = 128
BATCH, SEQ, DIM = 8, 256, 512
TOKENS = BATCH * SEQ
TILES = TOKENS // P
KT = DIM // P
CHUNK = 512
CHUNKS = TOKENS // CHUNK
CT = CHUNK // P

EXPERTS, INTER, GROUPS_R = 16, 128, 4
SLICES = EXPERTS + 2
W_UP, W_DOWN = KT * INTER, DIM
W_SLICE = 2 * W_UP + W_DOWN
RAW_SLICE = W_SLICE + 2

HEADS, KV, HD = 32, 8, 128
QPK = HEADS // KV
W_QKV = (QPK + 2) * DIM
W_O = QPK * DIM
EPS = 1e-5
RING = 4
SLOT_TILES = -(-(2 * TILES + EXPERTS - 1) // RING) * RING
TRI_AT = 3 * P + 2 * SEQ
BIG = 1e30
PARTS = ((0, 0), (0, 1), (1, 0))


def bc(ap, shape):
    return ap.unsqueeze(len(shape) - 1).to_broadcast(list(shape))


class Semaphores:

    def __init__(self, nc, ctx, tag):
        self.nc, self.ctx, self.tag, self.all = nc, ctx, tag, []

    def __call__(self, name):
        self.all.append(self.ctx.enter_context(self.nc.semaphore(name + self.tag)))
        return self.all[-1]

    def clear(self):
        with self.nc.Block() as block:
            @block.gpsimd
            def _(pool):
                for s in self.all:
                    pool.sem_clear(s)


def each(eng, count, body):
    body(0)
    with eng.Fori(1, count) as i:
        body(i)


def normalise(nc, ctx, sem, tag, X, XT, ident, work, moments, start, router_w=None, logits=None,
              router_in=None, x_in=None, ident_in=None, zeros=None):
    mean_var, rstd = moments
    xn, xt = work
    split = len(XT) == 2
    stats = ctx.enter_context(nc.sbuf_tensor(f"stats{tag}", [P, TILES, 6], F32))
    std = ctx.enter_context(nc.sbuf_tensor(f"std{tag}", [P, TILES], F32))
    eps = ctx.enter_context(nc.sbuf_tensor(f"eps{tag}", [P, 1], F32))

    stats_done, aggr_done, std_done, rstd_done = sem("stats_done"), sem("aggr_done"), sem("std_done"), sem("rstd_done")
    xn_ready, turned, high_ready, second_ready = (
        sem("xn_ready"), sem("turned"), sem("high_ready"), sem("second_ready"))
    eps_set, routed = sem("eps_set"), sem("routed")

    with ExitStack() as inner:
        bank = [inner.enter_context(nc.psum_tensor(f"turn{i}{tag}", [P, KT, P], F32)) for i in range(2)]
        block = inner.enter_context(nc.Block())

        def is_first(t):
            return isinstance(t, int) and t == 0

        @block.vector
        def _(dve):
            dve.memset(eps[:], EPS).then_inc(eps_set, 1)
            for t in range(TILES):
                if x_in is not None and t % CT == 0:
                    dve.wait_ge(x_in[t // CT], 16)
                dve.bn_stats(stats[:, t, :], X[:, t, :]).then_inc(stats_done, 1)
            for t in range(TILES):
                dve.wait_ge(stats_done, t + 1)
                dve.bn_aggr(mean_var[:, t, :], stats[:, t, :]).then_inc(aggr_done, 1)
            dve.wait_ge(std_done, 1)
            dve.reciprocal(rstd[:], std[:]).then_inc(rstd_done, 1)
            dve.wait_ge(rstd_done, 1)

            def second(t):
                for b in range(2):
                    cols = bass.ds((t + b) * P, P)
                    dve.wait_ge(high_ready, t + b + 1)
                    if split:
                        dve.tensor_tensor(XT[1][:, :, cols], bank[b][:], XT[0][:, :, cols].bitcast(F32),
                                          ALU.subtract).then_inc(second_ready, 1)
                    else:
                        dve.wait_ge(routed, t)
                        dve.tensor_copy(xt[:, b, :].rearrange("p (k n) -> p k n", k=KT), XT[0][:, :, cols]).then_inc(second_ready, 1)

            def two_tiles(pair):
                t = pair * 2
                for b in range(2):
                    dve.wait_ge(turned, t)
                    dve.tensor_scalar(xn[:, b, :], X[:, t + b, :], mean_var[:, t + b, 0:1], rstd[:, bass.ds(t + b, 1)],
                                      ALU.subtract, ALU.mult).then_inc(xn_ready, 1)
                if not is_first(t):
                    second(t - 2)
            each(dve, TILES // 2, two_tiles)
            second(TILES - 2)

        if zeros is not None:
            @block.gpsimd
            def _(pool):
                pool.memset(zeros[0][:], 0.0).then_inc(zeros[1], 1)

        @block.scalar
        def _(act):
            act.wait_ge(eps_set, 1)
            act.wait_ge(aggr_done, TILES)
            act.activation(std[:], mean_var[:, :, 1], ACT.Sqrt, bias=eps[:, 0:1]).then_inc(std_done, 1)

            def two_tiles(pair):
                t = pair * 2
                for b in range(2):
                    act.wait_ge(turned, t + b + 1)
                    act.activation(XT[0][:, :, bass.ds((t + b) * P, P)], bank[b][:], ACT.Copy).then_inc(high_ready, 1)
            each(act, TILES // 2, two_tiles)

        if start:
            block.sync(start)

        @block.tensor
        def _(pe):
            def route(t):
                for b in range(2):
                    pe.wait_ge(second_ready, t + b + 1)
                    for k in range(KT):
                        last = pe.matmul(logits[:, bass.ds((t + b) * EXPERTS, EXPERTS)], xt[:, b, k * P:(k + 1) * P],
                                         router_w[:, k, :], start=(k == 0), stop=(k == KT - 1))
                    last.then_inc(routed, 1)

            def two_tiles(pair):
                t = pair * 2
                for b in range(2):
                    pe.wait_ge(xn_ready, t + b + 1)
                    pe.wait_ge(second_ready if split else high_ready, t)
                    for k in range(KT):
                        last = pe.transpose(bank[b][:, k, :], xn[:, b, k * P:(k + 1) * P], ident[:])
                    last.then_inc(turned, 1)
                if router_w is not None and not is_first(t):
                    route(t - 2)
            if ident_in is not None:
                pe.wait_ge(ident_in, 16)
            if router_w is not None:
                pe.wait_ge(router_in, 16)
            each(pe, TILES // 2, two_tiles)
            if router_w is not None:
                route(TILES - 2)


def route_and_share(nc, ctx, sem, pool_sem, tag, X, XT, moments, logits, rows, tri, tile_index, ident, weights, routed, xslots, shared_in, filled):
    mean_var, rstd = moments
    shared_w, shared_b, b3 = weights
    pos, half_gate, tile_expert = routed
    n = TILES * EXPERTS
    G3 = (P, TILES, GROUPS_R)
    E3 = (P, TILES, EXPERTS)
    three = "p (t e) -> p t e"

    def sb(name, shape, dt=F32):
        return ctx.enter_context(nc.sbuf_tensor(name + tag, shape, dt))

    lg, ex, sc, eq, cand, one2 = (sb(x, [P, TILES, EXPERTS]) for x in ("lg", "ex", "sc", "eq", "cand", "one2"))
    ms, picks, one = ex, eq, [lg, one2]
    chosen = sb("chosen", [P, TILES + 1, EXPERTS])
    gmax, geq, gcand, keep1, keep2, gleft, pen = (
        sb(x, [P, TILES, GROUPS_R]) for x in ("gmax", "geq", "gcand", "keep1", "keep2", "gleft", "pen"))
    m, total, inv, m1, low = (sb(x, [P, TILES]) for x in ("m", "total", "inv", "m1", "low"))
    count, whole, tiles_e, upto, base = (sb(x, [P, EXPERTS]) for x in ("count", "whole", "tiles_e", "upto", "base"))
    whole_i = sb("whole_i", [P, EXPERTS], mybir.dt.int32)
    ones_row = sb("ones_row", [P, P])
    owner = sb("owner", [P, SLOT_TILES])
    xn = sb("xn", [P, RING, DIM])
    before = xn[:].rearrange("p r d -> p (r d)")[:, 0:SLOT_TILES * EXPERTS].rearrange("p (s e) -> p s e", e=EXPERTS)
    gates = sb("gates", [P, 2, CHUNK])
    silu, prod = (sb(x, [P, 2, CHUNK]) for x in ("silu", "prod"))
    lin = prod

    step, shifted, exped, chosen_ready, ones_set, counted = (
        sem("step"), sem("shifted"), sem("exped"), sem("chosen_ready"), sem("ones_set"), sem("counted"))
    gates_ready, gates_turned, gates_copied, gates_ones = sem("gates_ready"), sem("gates_turned"), sem("gates_copied"), sem("gates_ones")
    routed_ready, xn_ready = sem("routed_ready"), sem("xn_again")
    sent = [pool_sem(f"sent{i}_") for i in range(RING)]
    up1_done, up2_done, silu_done, lin_done, prod_done, y_done, y_added = (
        sem("up1_done"), sem("up2_done"), sem("silu_done"), sem("lin_done"), sem("prod_done"), sem("y_done"), sem("y_added"))

    with ExitStack() as inner:
        def bank(name, shape):
            return inner.enter_context(nc.psum_tensor(name + tag, shape, F32))
        up1 = [bank(f"up1_{j}", [P, CHUNK]) for j in range(2)]
        up2 = bank("up2", [P, CHUNK])
        y = [bank(f"y{t}", [P, DIM]) for t in range(CT)]
        block = inner.enter_context(nc.Block())

        @block.vector
        def _(dve):
            done = [0]

            def link(ins):
                done[0] += 1
                ins.then_inc(step, 1)
                dve.wait_ge(step, done[0])

            def first_max(values, marks, equal, candidate, idx, shape):
                link(dve.tensor_reduce(m1[:], values, AX_X, ALU.max))
                link(dve.tensor_tensor(equal, values, bc(m1[:], shape), ALU.is_equal))
                link(dve.tensor_tensor(candidate, equal, idx, ALU.mult))
                link(dve.tensor_reduce(low[:], candidate, AX_X, ALU.min))
                link(dve.tensor_tensor(marks, candidate, bc(low[:], shape), ALU.is_equal))

            idx_e = rows[:, 2, 0:EXPERTS].unsqueeze(1).to_broadcast(list(E3))
            idx_g = rows[:, 2, 0:GROUPS_R].unsqueeze(1).to_broadcast(list(G3))
            dve.memset(ones_row[:], 1.0).then_inc(ones_set, 1)
            dve.memset(chosen[:, TILES, :], 0.0).then_inc(ones_set, 1)
            dve.memset(gates[0:EXPERTS + 1, :, :], 1.0).then_inc(gates_ones, 1)
            link(dve.tensor_tensor(lg[:], logits[:, 0:n].rearrange(three, t=TILES), rows[:, 0, :].unsqueeze(1).to_broadcast(list(E3)), ALU.add))
            link(dve.tensor_reduce(m[:], lg[:], AX_X, ALU.max))
            dve.tensor_tensor(lg[:], lg[:], bc(m[:], E3), ALU.subtract).then_inc(shifted, 1)
            dve.wait_ge(exped, 1)
            link(dve.tensor_reduce(total[:], ex[:], AX_X, ALU.add))
            link(dve.reciprocal(inv[:], total[:]))
            link(dve.tensor_tensor(sc[:], ex[:], bc(inv[:], E3), ALU.mult))
            link(dve.tensor_tensor(sc[:], sc[:], rows[:, 1, :].unsqueeze(1).to_broadcast(list(E3)), ALU.add))
            by_group = "p t (g e) -> p t g e"
            link(dve.tensor_reduce(gmax[:], sc[:].rearrange(by_group, g=GROUPS_R), AX_X, ALU.max))
            first_max(gmax[:], keep1[:], geq[:], gcand[:], idx_g, G3)
            link(dve.scalar_tensor_tensor(gleft[:], keep1[:], -2 * BIG, gmax[:], ALU.mult, ALU.add))
            first_max(gleft[:], keep2[:], geq[:], gcand[:], idx_g, G3)
            link(dve.tensor_tensor(keep1[:], keep1[:], keep2[:], ALU.add))
            link(dve.tensor_scalar(pen[:], keep1[:], -1.0, BIG, ALU.add, ALU.mult))
            link(dve.tensor_tensor(ms[:].rearrange(by_group, g=GROUPS_R), sc[:].rearrange(by_group, g=GROUPS_R),
                                   bc(pen[:], (P, TILES, GROUPS_R, EXPERTS // GROUPS_R)), ALU.add))
            first_max(ms[:], one[0][:], eq[:], cand[:], idx_e, E3)
            link(dve.scalar_tensor_tensor(ms[:], one[0][:], -2 * BIG, ms[:], ALU.mult, ALU.add))
            first_max(ms[:], one[1][:], eq[:], cand[:], idx_e, E3)
            dve.tensor_tensor(chosen[:, 0:TILES, :], one[0][:], one[1][:], ALU.add).then_inc(chosen_ready, 1)
            dve.wait_ge(chosen_ready, 1)
            dve.tensor_tensor(picks[:], sc[:], chosen[:, 0:TILES, :], ALU.mult).then_inc(gates_ready, 1)
            for k in range(2):
                link(dve.tensor_tensor(cand[:], sc[:], one[k][:], ALU.mult))
                link(dve.tensor_reduce(total[:], cand[:], AX_X, ALU.add))
                link(dve.tensor_scalar(half_gate[:, k, :], total[:], 0.5, None, ALU.mult))
            dve.wait_ge(counted, 1)
            link(dve.tensor_scalar(whole[:], logits[:, n:n + EXPERTS], 1.0 / P, (P - 1.0) / P - 0.5 + 0.5 / P, ALU.mult, ALU.add))
            link(dve.tensor_copy(whole_i[:], whole[:]))
            link(dve.tensor_copy(tiles_e[:], whole_i[:]))
            link(dve.tensor_tensor_scan(upto[:], ones_row[:, 0:EXPERTS], tiles_e[:], 0.0, ALU.mult, ALU.add))
            link(dve.tensor_tensor(base[:], upto[:], tiles_e[:], ALU.subtract))
            link(dve.tensor_scalar(base[:], base[:], float(P), None, ALU.mult))
            link(dve.tensor_tensor(ms[:], logits[:, 0:n].rearrange(three, t=TILES), base[:].unsqueeze(1).to_broadcast(list(E3)), ALU.add))
            for k in range(2):
                link(dve.tensor_tensor(cand[:], ms[:], one[k][:], ALU.mult))
                link(dve.tensor_reduce(total[:], cand[:], AX_X, ALU.add))
                dve.tensor_copy(pos[:, k, :], total[:]).then_inc(routed_ready, 1)
            link(dve.tensor_tensor(before, upto[:].unsqueeze(1).to_broadcast([P, SLOT_TILES, EXPERTS]),
                                   bc(tile_index[:], (P, SLOT_TILES, EXPERTS)), ALU.is_le))
            link(dve.tensor_reduce(owner[:], before, AX_X, ALU.add))
            dve.tensor_scalar(tile_expert[:], owner[:], EXPERTS - 1.0, None, ALU.min).then_inc(routed_ready, 1)
            for c in range(CHUNKS):
                dve.wait_ge(gates_turned, c + 1)
                dve.wait_ge(gates_ones, 1)
                if c >= 2:
                    dve.wait_ge(y_done, (c - 1) * CT)
                dve.tensor_copy(gates[0:EXPERTS, c % 2, :], logits[0:EXPERTS, :]).then_inc(gates_copied, 1)
                for t in range(c * CT, (c + 1) * CT):
                    if t >= RING:
                        dve.wait_ge(sent[t % RING], 32 * (t // RING))
                    dve.tensor_scalar(xn[:, t % RING, :], X[:, t, :], mean_var[:, t, 0:1], rstd[:, t:t + 1],
                                      ALU.subtract, ALU.mult).then_inc(xn_ready, 1)
                dve.wait_ge(xn_ready, (c + 1) * CT)
                for t in range(CT):
                    dve.wait_ge(y_done, c * CT + t + 1)
                    dve.scalar_tensor_tensor(X[:, c * CT + t, :], y[t][:], 0.5, X[:, c * CT + t, :],
                                             ALU.mult, ALU.add).then_inc(y_added, 1)

        @block.gpsimd
        def _(pool):
            def products(c):
                for j in range(2):
                    s = 2 * c + j
                    pool.wait_ge(silu_done, s + 1)
                    pool.wait_ge(lin_done, s + 1)
                    pool.tensor_tensor(prod[:, j, :], silu[:, j, :], lin[:, j, :], ALU.mult).then_inc(prod_done, 1)

            products(0)
            pool.wait_ge(filled, 16)
            for c in range(CHUNKS):
                for t in range(c * CT, (c + 1) * CT):
                    pool.wait_ge(routed_ready, 2)
                    pool.wait_ge(xn_ready, t + 1)
                    for k in range(2):
                        pool.indirect_dma_start(xslots, bass.IndirectOffsetOnAxis(ap=pos[:, k, t:t + 1], axis=0),
                                                xn[:, t % RING, :], None).then_inc(sent[t % RING], 16)
                if c + 1 < CHUNKS:
                    products(c + 1)
            for i in range(RING):
                pool.wait_ge(sent[i], 32 * (TILES // RING))

        @block.scalar
        def _(act):
            act.wait_ge(shifted, 1)
            act.activation(ex[:], lg[:], ACT.Exp).then_inc(exped, 1)
            act.wait_ge(shared_in, 48)
            for c in range(CHUNKS):
                for j in range(2):
                    s = 2 * c + j
                    act.wait_ge(up1_done, s + 1)
                    if c:
                        act.wait_ge(prod_done, s - 1)
                    act.activation(silu[:, j, :], up1[j][:], ACT.Silu, bias=shared_b[:, j, 0:1]).then_inc(silu_done, 1)
                    act.wait_ge(up2_done, s + 1)
                    if c:
                        act.wait_ge(y_done, c * CT)
                    act.activation(lin[:, j, :], up2[:], ACT.Identity, bias=shared_b[:, j, 1:2]).then_inc(lin_done, 1)

        @block.tensor
        def _(pe):
            def up(c, j):
                s = 2 * c + j
                if s >= 2:
                    pe.wait_ge(silu_done, s - 1)
                for bank_, at, done in ((up1[j], 0, up1_done), (up2, W_UP, up2_done)):
                    if bank_ is up2 and s:
                        pe.wait_ge(lin_done, s)
                    for k in range(KT):
                        last = pe.matmul(bank_[:], shared_w[:, j, at + k * P:at + (k + 1) * P], XT[:, k, c * CHUNK:(c + 1) * CHUNK],
                                         start=(k == 0), stop=(k == KT - 1))
                    last.then_inc(done, 1)

            def down(c):
                if c:
                    pe.wait_ge(y_added, c * CT)
                pe.wait_ge(gates_copied, c + 1)
                for t in range(CT):
                    pe.matmul(y[t][:], gates[0:EXPERTS + 1, c % 2, t * P:(t + 1) * P], b3[0:EXPERTS + 1, :],
                              start=True, stop=False)
                    for j in range(2):
                        pe.wait_ge(prod_done, 2 * c + j + 1)
                        last = pe.matmul(y[t][:], prod[:, j, t * P:(t + 1) * P], shared_w[:, j, 2 * W_UP:W_SLICE],
                                         start=False, stop=(j == 1))
                    last.then_inc(y_done, 1)

            pe.wait_ge(shared_in, 48)
            up(0, 0)
            up(0, 1)
            pe.wait_ge(ones_set, 2)
            pe.wait_ge(chosen_ready, 1)
            pe.matmul(logits[:, 0:n + EXPERTS], tri[:], chosen[:].rearrange("p t e -> p (t e)"), start=True, stop=False)
            for t in range(TILES):
                last = pe.matmul(logits[:, (t + 1) * EXPERTS:n + EXPERTS].rearrange(three, e=EXPERTS), ones_row[:],
                                 chosen[:, t, :].unsqueeze(1).to_broadcast([P, TILES - t, EXPERTS]),
                                 start=False, stop=(t == TILES - 1))
            last.then_inc(counted, 1)
            pe.wait_ge(gates_ready, 1)
            pe.wait_ge(routed_ready, 2)
            for c in range(CHUNKS):
                if c:
                    up(c, 0)
                    up(c, 1)
                    pe.wait_ge(gates_copied, c)
                for i in range(CT):
                    last = pe.transpose(logits[0:EXPERTS, i * P:(i + 1) * P], picks[:, c * CT + i, :], ident[:])
                last.then_inc(gates_turned, 1)
                down(c)


def run_experts(nc, ctx, sem, pool_sem, tag, ident, W, w_in, b12, b12_in, tile_expert, xslots, yslots):
    def sb(name, shape, dt=F32):
        return ctx.enter_context(nc.sbuf_tensor(name + tag, shape, dt))

    xg, xgt = sb("xg", [P, RING, DIM]), sb("xgt", [P, 2, KT, P])
    act_in, silu, h, ht, yo = sb("act_in", [P, 2, 2 * INTER]), sb("silu_e", [P, 2, INTER]), sb("h", [P, 2, INTER]), sb("ht", [P, 2, P]), sb("yo", [P, RING, DIM])
    x_in = [sem(f"slots_in{i}_") for i in range(RING)]
    y_out = [pool_sem(f"slots_out{i}_") for i in range(RING)]
    turned, xt_copied, upped, biased, silued, multiplied, h_turned, h_copied, downed, y_copied = (
        sem("e_" + x) for x in "turned xt_copied upped biased silued multiplied h_turned h_copied downed y_copied".split())

    with ExitStack() as inner:
        def bank(name, width):
            return [inner.enter_context(nc.psum_tensor(f"{name}{i}{tag}", [P, CHUNK], F32))[:, 0:width] for i in range(2)]
        xt_bank = [b.rearrange("p (k n) -> p k n", k=KT) for b in bank("xtb", DIM)]
        up_bank, ht_bank, y_bank = bank("upb", 2 * INTER), bank("htb", P), bank("yb", DIM)
        block = inner.enter_context(nc.Block())

        def rounds(eng, step):
            def body(i):
                for r in range(RING):
                    step(i * RING + r, r)
            each(eng, SLOT_TILES // RING, body)

        @block.sync
        def _(sp):
            def step(j, r):
                if not (isinstance(j, int) and j < RING):
                    sp.wait_ge(turned, j - RING + 1)
                sp.dma_start(xg[:, r, :], xslots[bass.ds(j * P, P), :]).then_inc(x_in[r], 16)
            rounds(sp, step)

        @block.gpsimd
        def _(pool):
            def step(j, r):
                pool.wait_ge(y_copied, j + 1)
                pool.dma_start(yslots[bass.ds(j * P, P), :], yo[:, r, :]).then_inc(y_out[r], 16)
            rounds(pool, step)
            for r in range(RING):
                pool.wait_ge(y_out[r], 16 * (SLOT_TILES // RING))

        @block.tensor
        def _(pe):
            def turn(j, r):
                pe.wait_ge(x_in[r], 16 * (j // RING + 1) if isinstance(j, int) else 16 * (j // RING) + 16)
                if not (isinstance(j, int) and j < 2):
                    pe.wait_ge(xt_copied, j - 1)
                for k in range(KT):
                    last = pe.transpose(xt_bank[r % 2][:, k, :], xg[:, r, k * P:(k + 1) * P], ident[:])
                last.then_inc(turned, 1)

            def up(j, b):
                e = pe.value_load(tile_expert[0:1, bass.ds(j, 1)], min_val=0, max_val=EXPERTS - 1)
                pe.wait_ge(xt_copied, j + 1)
                if not (isinstance(j, int) and j < 2):
                    pe.wait_ge(biased, j - 1)
                for k in range(KT):
                    last = pe.matmul(up_bank[b], xgt[:, b, k, :], W[:, e, 2 * k * INTER:2 * (k + 1) * INTER],
                                     start=(k == 0), stop=(k == KT - 1))
                last.then_inc(upped, 1)

            def turn_hidden(j, b):
                pe.wait_ge(multiplied, j + 1)
                if not (isinstance(j, int) and j < 2):
                    pe.wait_ge(h_copied, j - 1)
                pe.transpose(ht_bank[b], h[:, b, :], ident[:]).then_inc(h_turned, 1)

            def down(j, b):
                e = pe.value_load(tile_expert[0:1, bass.ds(j, 1)], min_val=0, max_val=EXPERTS - 1)
                pe.wait_ge(h_copied, j + 1)
                if not (isinstance(j, int) and j < 2):
                    pe.wait_ge(y_copied, j - 1)
                pe.matmul(y_bank[b], ht[:, b, :], W[:, e, 2 * W_UP:W_SLICE], start=True, stop=True).then_inc(downed, 1)

            def step(j, r):
                turn(j, r)
                if not (isinstance(j, int) and j < 2):
                    turn_hidden(j - 2, r % 2)
                if not (isinstance(j, int) and j < 1):
                    up(j - 1, (r + 1) % 2)
                if not (isinstance(j, int) and j < 2):
                    down(j - 2, r % 2)
            pe.wait_ge(w_in, 16 * EXPERTS)
            rounds(pe, step)
            turn_hidden(SLOT_TILES - 2, 0)
            up(SLOT_TILES - 1, 1)
            down(SLOT_TILES - 2, 0)
            turn_hidden(SLOT_TILES - 1, 1)
            down(SLOT_TILES - 1, 1)

        @block.scalar
        def _(act):
            def silu_of(j, b):
                act.wait_ge(biased, j + 1)
                if not (isinstance(j, int) and j < 2):
                    act.wait_ge(multiplied, j - 1)
                act.activation(silu[:, b, :], act_in[:, b, 0:INTER], ACT.Silu).then_inc(silued, 1)

            def copy_out(j, r):
                act.wait_ge(downed, j + 1)
                if not (isinstance(j, int) and j < RING):
                    act.wait_ge(y_out[r], 16 * (j // RING))
                act.activation(yo[:, r, :], y_bank[r % 2], ACT.Copy).then_inc(y_copied, 1)

            def step(j, r):
                act.wait_ge(turned, j + 1)
                if not (isinstance(j, int) and j < 2):
                    act.wait_ge(upped, j - 1)
                act.activation(xgt[:, r % 2, :, :], xt_bank[r % 2], ACT.Copy).then_inc(xt_copied, 1)
                if not (isinstance(j, int) and j < 1):
                    silu_of(j - 1, (r + 1) % 2)
                if not (isinstance(j, int) and j < 2):
                    copy_out(j - 2, (r - 2) % RING)
            rounds(act, step)
            silu_of(SLOT_TILES - 1, 1)
            copy_out(SLOT_TILES - 2, RING - 2)
            copy_out(SLOT_TILES - 1, RING - 1)

        @block.vector
        def _(dve):
            def hidden(j, b):
                e = dve.value_load(tile_expert[0:1, bass.ds(j, 1)], min_val=0, max_val=EXPERTS - 1)
                dve.wait_ge(upped, j + 1)
                if not (isinstance(j, int) and j < 2):
                    dve.wait_ge(multiplied, j - 1)
                dve.tensor_tensor(act_in[:, b, :], up_bank[b], b12[:, e, :], ALU.add).then_inc(biased, 1)
                dve.wait_ge(silued, j + 1)
                dve.wait_ge(biased, j + 1)
                if not (isinstance(j, int) and j < 2):
                    dve.wait_ge(h_turned, j - 1)
                dve.tensor_tensor(h[:, b, :], silu[:, b, :], act_in[:, b, INTER:2 * INTER], ALU.mult).then_inc(multiplied, 1)

            def copy_turned(j, b):
                dve.wait_ge(h_turned, j + 1)
                if not (isinstance(j, int) and j < 2):
                    dve.wait_ge(downed, j - 1)
                dve.tensor_copy(ht[:, b, :], ht_bank[b]).then_inc(h_copied, 1)

            def step(j, r):
                if not (isinstance(j, int) and j < 2):
                    copy_turned(j - 2, r % 2)
                if not (isinstance(j, int) and j < 1):
                    hidden(j - 1, (r + 1) % 2)
            dve.wait_ge(b12_in, 16)
            rounds(dve, step)
            copy_turned(SLOT_TILES - 2, 0)
            hidden(SLOT_TILES - 1, 1)
            copy_turned(SLOT_TILES - 1, 1)


def combine(nc, ctx, sem, pool_sem, tag, X, pos, half_gate, yslots, out_dram):
    got = ctx.enter_context(nc.sbuf_tensor("got" + tag, [P, RING, 2, DIM], F32))
    landed = [pool_sem(f"landed{i}_") for i in range(RING)]
    first_added, added, stored = sem("first_added"), sem("both_added"), sem("stored")
    with nc.Block() as block:
        @block.gpsimd
        def _(pool):
            for t in range(TILES):
                if t >= RING:
                    pool.wait_ge(added, t - RING + 1)
                for k in range(2):
                    pool.indirect_dma_start(got[:, t % RING, k, :], None, yslots,
                                            bass.IndirectOffsetOnAxis(ap=pos[:, k, t:t + 1], axis=0)).then_inc(landed[t % RING], 16)

        @block.vector
        def _(dve):
            def add(t, k, done):
                dve.scalar_tensor_tensor(X[:, t, :], got[:, t % RING, k, :], half_gate[:, k, t:t + 1], X[:, t, :],
                                         ALU.mult, ALU.add).then_inc(done, 1)
            for t in range(TILES):
                dve.wait_ge(landed[t % RING], 32 * (t // RING + 1))
                add(t, 0, first_added)
                dve.wait_ge(first_added, t + 1)
                add(t, 1, added)

        @block.sync
        def _(sp):
            if out_dram is not None:
                for t in range(TILES):
                    sp.wait_ge(added, t + 1)
                    sp.dma_start(out_dram[:, t, :], X[:, t, :]).then_inc(stored, 16)
                sp.wait_ge(stored, 16 * TILES)


def attention(nc, ctx, sem, X, XT, ident, a_dram, loads, loaded):
    def sb(name, shape, dt=F32):
        return ctx.enter_context(nc.sbuf_tensor(name, shape, dt))

    Wqkv = [sb("wqkv_high", [P, W_QKV], F32R), sb("wqkv_low", [P, W_QKV], F32R)]
    Wo = [sb("wo_high", [P, W_O], F32R), sb("wo_low", [P, W_O], F32R)]
    swapped, straight = sb("swapped", [P, 2, CHUNK]), sb("straight", [P, 2, CHUNK])
    qk = sb("qk", [P, QPK + 1, CHUNK])
    v_turned, v = sb("v_turned", [P, CHUNK]), sb("v", [P, CT, HD])
    probs, probs_t = sb("probs", [P, 2, QPK, P]), sb("probs_t", [P, 2, QPK * P])
    row_max, row_sum, row_inv = sb("row_max", [P, 2, QPK]), sb("row_sum", [P, 2, QPK]), sb("row_inv", [P, 2, QPK])
    heads_out = [sb("heads_high", [P, QPK, CHUNK], F32R), sb("heads_low", [P, QPK, CHUNK], F32R)]

    raw_qkv, raw_o, rotary, masks = loads
    raw_qkv_in, raw_o_in, consts_in = loaded
    names = ("qkv_high qkv_low o_high o_low proj_done swap_done rope_mul rope_sin rope_add "
             "vt_copied v_turned_back v_copied scored masked max_done sub_done exp_done sum_done inv_done p_ready "
             "p_turned pt_copied pv_done oh_done ol_done wo_done added").split()
    s = {name: sem("a_" + name) for name in names}
    (qkv_high, qkv_low, o_high, o_low, proj_done, swap_done, rope_mul, rope_sin, rope_add,
     vt_copied, v_back, v_copied, scored, masked, max_done, sub_done, exp_done, sum_done, inv_done, p_ready,
     p_turned, pt_copied, pv_done, oh_done, ol_done, wo_done, added) = [s[x] for x in names]
    ROPES, PROJ = QPK + 1, QPK + 2
    NCH = KV * CHUNKS
    scale = float(HD) ** -0.5
    H = HD // 2

    with ExitStack() as inner:
        def bank(name, shape):
            return inner.enter_context(nc.psum_tensor(name, shape, F32))
        proj = [bank(f"proj{i}", [P, CHUNK]) for i in range(2)]
        score = [bank(f"score{i}", [P, QPK, P]) for i in range(2)]
        turn = bank("turn", [P, CT, P])
        pv = bank("pv", [P, QPK * P])
        yo = [bank(f"yo{i}", [P, DIM]) for i in range(2)]

        def mix_bank(u):
            return (pv if u % 2 == 0 else proj[1])[:]

        def turn_bank(u):
            return (score[0] if u == 3 else turn)[:]

        block = inner.enter_context(nc.Block())

        @block.sync
        def _(sp):
            with sp.Fori(1, KV) as g:
                sp.wait_ge(qkv_low, PROJ * g)
                sp.dma_start(raw_qkv[:], a_dram[g, :, 0:W_QKV]).then_inc(raw_qkv_in, 16)
                sp.wait_ge(o_low, QPK * g)
                sp.dma_start(raw_o[:], a_dram[g, :, W_QKV:W_QKV + W_O]).then_inc(raw_o_in, 16)

        @block.tensor
        def _(pe):
            def project(n, g, c, i):
                pe.wait_ge(qkv_low, PROJ * g + i + 1)
                if i == 1:
                    pe.wait_ge(vt_copied, n)
                    pe.wait_ge(ol_done, CT * n)
                else:
                    pe.wait_ge(rope_mul, ROPES * n + max(i - 1, 0))
                for k in range(KT):
                    for m, (a, b) in enumerate(PARTS):
                        last = pe.matmul(proj[i % 2][:], Wqkv[a][:, i * DIM + k * P:i * DIM + (k + 1) * P],
                                         XT[b][:, k, bass.ds(c * CHUNK, CHUNK)],
                                         start=(k == 0 and m == 0), stop=(k == KT - 1 and m == 2))
                last.then_inc(proj_done, 1)

            def out_proj(n, g, t):
                pe.wait_ge(o_low, QPK * g + QPK)
                pe.wait_ge(ol_done, CT * n + t + 1)
                pe.wait_ge(added, CT * n + max(t - 1, 0))
                for h in range(QPK):
                    for m, (a, b) in enumerate(PARTS):
                        last = pe.matmul(yo[t % 2][:], heads_out[a][:, h, t * P:(t + 1) * P], Wo[b][:, h * DIM:(h + 1) * DIM],
                                         start=(h == 0 and m == 0), stop=(h == QPK - 1 and m == 2))
                last.then_inc(wo_done, 1)

            def turn_v(n):
                pe.wait_ge(vt_copied, n + 1)
                pe.wait_ge(pt_copied, CT * n)
                for t in range(CT):
                    last = pe.transpose(turn[:, t, :], v_turned[:, t * P:(t + 1) * P], ident[:])
                last.then_inc(v_back, 1)

            def scores(n, u):
                pe.wait_ge(rope_add, ROPES * (n + 1))
                pe.wait_ge(masked, CT * n + max(u - 1, 0))
                key_tile = u ^ 1
                for h in range(QPK):
                    last = pe.matmul(score[u % 2][:, h, :], qk[:, 1 + h, u * P:(u + 1) * P],
                                     qk[:, 0, key_tile * P:(key_tile + 1) * P], start=True, stop=True)
                last.then_inc(scored, 1)

            def turn_probs(n, u):
                pe.wait_ge(p_ready, CT * n + u + 1)
                if u == 0:
                    pe.wait_ge(v_copied, n + 1)
                elif u == 3:
                    pe.wait_ge(masked, CT * n + 3)
                else:
                    pe.wait_ge(pt_copied, CT * n + u)
                for h in range(QPK):
                    last = pe.transpose(turn_bank(u)[:, h, :], probs[:, u % 2, h, :], ident[:])
                last.then_inc(p_turned, 1)

            def mix(n, u):
                pe.wait_ge(pt_copied, CT * n + u + 1)
                pe.wait_ge(ol_done, CT * n + max(u - 1, 0))
                pe.matmul(mix_bank(u), v[:, u ^ 1, :], probs_t[:, u % 2, :],
                          start=True, stop=True).then_inc(pv_done, 1)

            def chunk(n, g, c, before):
                for i in range(PROJ):
                    project(n, g, c, i)
                if before:
                    out_proj(*before, 0)
                turn_v(n)
                scores(n, 0)
                scores(n, 1)
                if before:
                    out_proj(*before, 1)
                    out_proj(*before, 2)
                turn_probs(n, 0)
                scores(n, 2)
                turn_probs(n, 1)
                scores(n, 3)
                mix(n, 0)
                mix(n, 1)
                if before:
                    out_proj(*before, 3)
                turn_probs(n, 2)
                turn_probs(n, 3)
                mix(n, 2)
                mix(n, 3)

            chunk(0, 0, 0, None)
            with pe.Fori(1, NCH) as n:
                chunk(n, n // CHUNKS, n % CHUNKS, (n - 1, (n - 1) // CHUNKS))
            for t in range(CT):
                out_proj(NCH - 1, KV - 1, t)

        def by_head(eng, body, split_qkv, split_o):
            for i in range(PROJ):
                split_qkv(0, i)

            def head(g, last):
                body(g * CHUNKS, lambda u: None)
                for h in range(QPK):
                    split_o(g, h)
                with eng.Fori(1, CHUNKS - 1) as c:
                    body(g * CHUNKS + c, lambda u: None)

                def after(u):
                    if not last and u < 3:
                        split_qkv(g + 1, 2 * u)
                        split_qkv(g + 1, 2 * u + 1)
                body(g * CHUNKS + CHUNKS - 1, after)

            each(eng, KV - 1, lambda g: head(g, False))
            head(KV - 1, True)

        @block.scalar
        def _(act):
            def split_qkv(g, i):
                act.wait_ge(raw_qkv_in, 16 * (g + 1))
                if not (isinstance(g, int) and g == 0):
                    act.wait_ge(proj_done, PROJ * CHUNKS * g - PROJ + i + 1)
                act.activation(Wqkv[0][:, i * DIM:(i + 1) * DIM], raw_qkv[:, i * DIM:(i + 1) * DIM], ACT.Copy).then_inc(qkv_high, 1)

            def split_o(g, h):
                act.wait_ge(raw_o_in, 16 * (g + 1))
                act.wait_ge(wo_done, CHUNKS * CT * g)
                act.activation(Wo[0][:, h * DIM:(h + 1) * DIM], raw_o[:, h * DIM:(h + 1) * DIM], ACT.Copy).then_inc(o_high, 1)

            def body(n, after):
                for r in range(ROPES):
                    act.wait_ge(proj_done, PROJ * n + r + 1)
                    act.wait_ge(rope_add, ROPES * n + max(r - 1, 0))
                    act.activation(swapped[0:H, r % 2, :], proj[r % 2][H:HD, :], ACT.Copy)
                    act.activation(swapped[H:HD, r % 2, :], proj[r % 2][0:H, :], ACT.Copy).then_inc(swap_done, 1)
                act.wait_ge(proj_done, PROJ * (n + 1))
                act.wait_ge(v_back, n)
                act.activation(v_turned[:], proj[1][:], ACT.Copy).then_inc(vt_copied, 1)
                act.wait_ge(v_back, n + 1)
                act.wait_ge(pv_done, CT * n)
                act.activation(v[:], turn[:], ACT.Copy).then_inc(v_copied, 1)

                def exp(u):
                    act.wait_ge(sub_done, CT * n + u + 1)
                    act.activation(probs[:, u % 2, :, :], probs[:, u % 2, :, :], ACT.Exp, scale=scale).then_inc(exp_done, 1)

                def copy_turned(u):
                    act.wait_ge(p_turned, CT * n + u + 1)
                    act.wait_ge(pv_done, CT * n + max(u - 1, 0))
                    act.activation(probs_t[:, u % 2, :], turn_bank(u).rearrange("p h q -> p (h q)"), ACT.Copy).then_inc(pt_copied, 1)

                def high(u):
                    act.wait_ge(pv_done, CT * n + u + 1)
                    act.activation(heads_out[0][:, :, u * P:(u + 1) * P], mix_bank(u).rearrange("p (h q) -> p h q", h=QPK), ACT.Copy).then_inc(oh_done, 1)

                exp(0)
                exp(1)
                copy_turned(0)
                copy_turned(1)
                high(0)
                after(0)
                exp(2)
                high(1)
                exp(3)
                copy_turned(2)
                copy_turned(3)
                after(1)
                high(2)
                after(2)
                high(3)

            by_head(act, body, split_qkv, split_o)

        @block.gpsimd
        def _(pool):
            def split_qkv(g, i):
                pool.wait_ge(qkv_high, PROJ * g + i + 1)
                cols = slice(i * DIM, (i + 1) * DIM)
                pool.tensor_tensor(Wqkv[1][:, cols], raw_qkv[:, cols], Wqkv[0][:, cols].bitcast(F32), ALU.subtract).then_inc(qkv_low, 1)

            def split_o(g, h):
                pool.wait_ge(o_high, QPK * g + h + 1)
                cols = slice(h * DIM, (h + 1) * DIM)
                pool.tensor_tensor(Wo[1][:, cols], raw_o[:, cols], Wo[0][:, cols].bitcast(F32), ALU.subtract).then_inc(o_low, 1)

            def body(n, after):
                for r in range(ROPES):
                    pool.wait_ge(swap_done, ROPES * n + r + 1)
                    part = swapped[:, r % 2, :].rearrange("p (b s) -> p b s", s=SEQ)
                    pool.tensor_tensor(part, part, rotary[:, 1, :].unsqueeze(1).to_broadcast([P, CHUNK // SEQ, SEQ]),
                                       ALU.mult).then_inc(rope_sin, 1)

                def subtract(u):
                    pool.wait_ge(max_done, CT * n + u + 1)
                    pool.tensor_tensor(probs[:, u % 2, :, :], probs[:, u % 2, :, :], bc(row_max[:, u % 2, :], (P, QPK, P)),
                                       ALU.subtract).then_inc(sub_done, 1)

                def divide(u):
                    pool.wait_ge(inv_done, CT * n + u + 1)
                    pool.tensor_tensor(probs[:, u % 2, :, :], probs[:, u % 2, :, :], bc(row_inv[:, u % 2, :], (P, QPK, P)),
                                       ALU.mult).then_inc(p_ready, 1)

                subtract(0)
                subtract(1)
                divide(0)
                divide(1)
                after(0)
                subtract(2)
                subtract(3)
                divide(2)
                divide(3)
                after(1)
                after(2)

            pool.wait_ge(consts_in, 32)
            by_head(pool, body, split_qkv, split_o)

        @block.vector
        def _(dve):
            def multiply(n, r):
                dve.wait_ge(swap_done, ROPES * n + r + 1)
                dve.wait_ge(rope_add, ROPES * n + max(r - 1, 0))
                dve.tensor_tensor(straight[:, r % 2, :].rearrange("p (b s) -> p b s", s=SEQ),
                                  proj[r % 2][:].rearrange("p (b s) -> p b s", s=SEQ),
                                  rotary[:, 0, :].unsqueeze(1).to_broadcast([P, CHUNK // SEQ, SEQ]), ALU.mult).then_inc(rope_mul, 1)

            def add_halves(n, r):
                dve.wait_ge(rope_sin, ROPES * n + r + 1)
                dve.wait_ge(rope_mul, ROPES * n + r + 1)
                dve.wait_ge(scored, CT * n)
                dve.tensor_tensor(qk[:, r, :], straight[:, r % 2, :], swapped[:, r % 2, :], ALU.add).then_inc(rope_add, 1)

            def mask_and_max(n, u):
                dve.wait_ge(scored, CT * n + u + 1)
                dve.wait_ge(p_turned, CT * n + max(u - 1, 0))
                dve.tensor_tensor(probs[:, u % 2, :, :], score[u % 2][:],
                                  masks[:, u % 2, :].unsqueeze(1).to_broadcast([P, QPK, P]), ALU.add).then_inc(masked, 1)
                dve.wait_ge(masked, CT * n + u + 1)
                dve.wait_ge(sub_done, CT * n + max(u - 1, 0))
                dve.tensor_reduce(row_max[:, u % 2, :], probs[:, u % 2, :, :], AX_X, ALU.max).then_inc(max_done, 1)

            def inverse_sum(n, u):
                dve.wait_ge(exp_done, CT * n + u + 1)
                dve.tensor_reduce(row_sum[:, u % 2, :], probs[:, u % 2, :, :], AX_X, ALU.add).then_inc(sum_done, 1)
                dve.wait_ge(sum_done, CT * n + u + 1)
                dve.wait_ge(p_ready, CT * n + max(u - 1, 0))
                dve.reciprocal(row_inv[:, u % 2, :], row_sum[:, u % 2, :]).then_inc(inv_done, 1)

            def low(n, u):
                dve.wait_ge(oh_done, CT * n + u + 1)
                dve.tensor_tensor(heads_out[1][:, :, u * P:(u + 1) * P], mix_bank(u).rearrange("p (h q) -> p h q", h=QPK),
                                  heads_out[0][:, :, u * P:(u + 1) * P].bitcast(F32), ALU.subtract).then_inc(ol_done, 1)

            def add_out(n, c, t):
                dve.wait_ge(wo_done, CT * n + t + 1)
                dve.tensor_tensor(X[:, c * CT + t, :], yo[t % 2][:], X[:, c * CT + t, :], ALU.add).then_inc(added, 1)

            def chunk(n, before):
                for r in range(ROPES):
                    multiply(n, r)
                    if r:
                        add_halves(n, r - 1)
                add_halves(n, ROPES - 1)
                if before:
                    add_out(*before, 0)
                mask_and_max(n, 0)
                mask_and_max(n, 1)
                inverse_sum(n, 0)
                inverse_sum(n, 1)
                if before:
                    add_out(*before, 1)
                    add_out(*before, 2)
                mask_and_max(n, 2)
                mask_and_max(n, 3)
                low(n, 0)
                inverse_sum(n, 2)
                low(n, 1)
                inverse_sum(n, 3)
                if before:
                    add_out(*before, 3)
                low(n, 2)
                low(n, 3)

            dve.wait_ge(consts_in, 32)
            chunk(0, None)
            with dve.Fori(1, NCH) as n:
                chunk(n, (n - 1, (n - 1) % CHUNKS))
            for t in range(CT):
                add_out(NCH - 1, CHUNKS - 1, t)


def macaron_block(nc, x, w_ffn, b12_dram, b3_dram, router_dram, rows_dram, w_attn, consts_dram, out):
    x_v = x.rearrange("(t p) d -> p t d", p=P)
    out_v = out.rearrange("(t p) d -> p t d", p=P)
    xslots = nc.dram_tensor("xslots", [SLOT_TILES * P, DIM], F32, kind="Internal").ap()
    yslots = nc.dram_tensor("yslots", [SLOT_TILES * P, DIM], F32, kind="Internal").ap()

    with ExitStack() as ctx:
        def sb(name, shape, dt=F32):
            return ctx.enter_context(nc.sbuf_tensor(name, shape, dt))
        X = sb("X", [P, TILES, DIM])
        ident = sb("ident", [P, P])
        filled = ctx.enter_context(nc.semaphore("filled"))
        x_in = [ctx.enter_context(nc.semaphore(f"x_in{c}")) for c in range(CHUNKS)]
        ident_in = ctx.enter_context(nc.semaphore("ident_in"))

        def ffn(tag, first, last):
            with ExitStack() as own:
                sem = Semaphores(nc, own, tag)
                pool_sem = Semaphores(nc, ctx, tag)

                def sb(name, shape, dt=F32, ctx=own):
                    return ctx.enter_context(nc.sbuf_tensor(name + tag, shape, dt))
                W = sb("w_experts", [P, EXPERTS, W_SLICE])
                pos = sb("pos", [P, 2, TILES], mybir.dt.uint32)
                half_gate = sb("half_gate", [P, 2, TILES])
                tile_expert = sb("tile_expert", [P, SLOT_TILES], mybir.dt.int32)
                zeroed, router_in = sem("zeroed"), sem("router_in")
                params_in, shared_in, w_in, b12_in = sem("params_in"), sem("shared_in"), sem("w_in"), sem("b12_in")
                with ExitStack() as early:
                    XT = sb("xt", [P, KT, TOKENS], ctx=early)
                    shared_w, shared_b = sb("shared_w", [P, 2, W_SLICE], ctx=early), sb("shared_b", [P, 2, 2], ctx=early)
                    b3, tri = sb("b3", [P, DIM], ctx=early), sb("tri", [P, P], ctx=early)
                    router_w, rows = sb("router_w", [P, KT, EXPERTS], ctx=early), sb("rows", [P, 3, EXPERTS], ctx=early)
                    tile_index = sb("tile_index", [P, SLOT_TILES], ctx=early)
                    logits = early.enter_context(nc.psum_tensor("logits" + tag, [P, CHUNK], F32))
                    moments = sb("mean_var", [P, TILES, 2], ctx=early), sb("rstd", [P, TILES], ctx=early)
                    def start(sp):
                        if first:
                            for c in range(CHUNKS):
                                sp.dma_start(X[:, c * CT:(c + 1) * CT, :], x_v[:, c * CT:(c + 1) * CT, :]).then_inc(x_in[c], 16)
                            sp.dma_start(ident[:], consts_dram[:, 0:P]).then_inc(ident_in, 16)
                        sp.dma_start(router_w[:], router_dram).then_inc(router_in, 16)
                        sp.dma_start(rows[:], rows_dram.partition_broadcast(P)).then_inc(params_in, 16)
                        sp.dma_start(b3[0:EXPERTS + 1, :], b3_dram).then_inc(params_in, 16)
                        sp.dma_start(tri[:], consts_dram[:, TRI_AT:TRI_AT + P]).then_inc(params_in, 16)
                        sp.dma_start(tile_index[:], consts_dram[:, TRI_AT + P:TRI_AT + P + SLOT_TILES]).then_inc(params_in, 16)
                        for j in range(2):
                            sp.dma_start(shared_w[:, j, :], w_ffn[EXPERTS + j, :, 0:W_SLICE]).then_inc(shared_in, 16)
                        sp.dma_start(shared_b[:], w_ffn[EXPERTS:SLICES, :, W_SLICE:RAW_SLICE].rearrange("j p b -> p j b")).then_inc(shared_in, 16)
                        if first:
                            sp.wait_ge(zeroed, 1)
                            sp.dma_start(xslots.rearrange("(j p) d -> p j d", p=P),
                                         zeros[:].unsqueeze(1).to_broadcast([P, SLOT_TILES, DIM])).then_inc(filled, 16)
                        for e in range(EXPERTS):
                            sp.dma_start(W[:, e, :], w_ffn[e, :, 0:W_SLICE]).then_inc(w_in, 16)
                        sp.wait_ge(params_in, 64)
                        if first:
                            sp.wait_ge(filled, 16)

                    with ExitStack() as turning:
                        work = [sb(x, [P, 2, CHUNK], ctx=turning) for x in ("n_xn", "n_xt")]
                        if first:
                            zeros = sb("zeros", [P, DIM], ctx=turning)
                        normalise(nc, turning, sem, tag, X, [XT], ident, work, moments, start, router_w, logits,
                                  router_in, x_in if first else None, ident_in if first else None, (zeros, zeroed) if first else None)
                    with ExitStack() as routing:
                        route_and_share(nc, routing, sem, pool_sem, tag, X, XT, moments, logits, rows, tri, tile_index, ident,
                                        (shared_w, shared_b, b3), (pos, half_gate, tile_expert), xslots, shared_in, filled)
                with ExitStack() as late:
                    b12 = sb("b12", [P, EXPERTS, 2 * INTER], ctx=late)
                    with nc.Block() as block:
                        @block.sync
                        def _(sp):
                            sp.dma_start(b12[:], b12_dram.partition_broadcast(P)).then_inc(b12_in, 16)
                    run_experts(nc, late, sem, pool_sem, tag, ident, W, w_in, b12, b12_in, tile_expert, xslots, yslots)
                with ExitStack() as late:
                    combine(nc, late, sem, pool_sem, tag, X, pos, half_gate, yslots, out_v if last else None)
                if not last:
                    sem.clear()

        ffn("_f1", True, False)
        with ExitStack() as own:
            sem = Semaphores(nc, own, "_a")
            def sb(name, shape, dt=F32, ctx=own):
                return ctx.enter_context(nc.sbuf_tensor(name, shape, dt))
            XT = [sb("xt_high", [P, KT, TOKENS], F32R), sb("xt_low", [P, KT, TOKENS], F32R)]
            raw_qkv, raw_o = sb("raw_qkv", [P, W_QKV]), sb("raw_o", [P, W_O])
            rotary, masks = sb("rotary", [P, 2, SEQ]), sb("masks", [P, 2, P])
            raw_qkv_in, raw_o_in, consts_in = sem("raw_qkv_in"), sem("raw_o_in"), sem("consts_in")

            def start(sp):
                halves = "p (a b) -> p a b"
                sp.dma_start(raw_qkv[:], w_attn[0, :, 0:W_QKV]).then_inc(raw_qkv_in, 16)
                sp.dma_start(raw_o[:], w_attn[0, :, W_QKV:W_QKV + W_O]).then_inc(raw_o_in, 16)
                sp.dma_start(rotary[:], consts_dram[:, P:P + 2 * SEQ].rearrange(halves, a=2)).then_inc(consts_in, 16)
                sp.dma_start(masks[:], consts_dram[:, P + 2 * SEQ:2 * SEQ + 3 * P].rearrange(halves, a=2)).then_inc(consts_in, 16)

            with ExitStack() as turning:
                xn = sb("a_xn", [P, 2, CHUNK], ctx=turning)
                moments = sb("a_mean_var", [P, TILES, 2], ctx=turning), sb("a_rstd", [P, TILES], ctx=turning)
                normalise(nc, turning, sem, "_a", X, XT, ident, (xn, None), moments, start)
            attention(nc, own, sem, X, XT, ident, w_attn, (raw_qkv, raw_o, rotary, masks), (raw_qkv_in, raw_o_in, consts_in))
            sem.clear()
        ffn("_f2", False, True)


def kernel(**inputs):
    import numpy as _np
    import concourse.bacc as _bacc
    from concourse import mybir as _mybir
    from concourse.bass_utils import run_bass_kernel_spmd as _run

    a = {k.replace("L0_", ""): _np.asarray(v) for k, v in inputs.items()}

    def up(w):
        return w.reshape(len(w), KT, P, -1).transpose(0, 2, 1, 3).reshape(len(w), P, -1)

    def halves(w):
        return w.reshape(DIM, 2, INTER).transpose(1, 0, 2)

    def heads(w, n):
        return w.reshape(KV, n // KV, HD, KT, P).transpose(0, 4, 1, 3, 2).reshape(KV, P, -1)

    experts_up = up(_np.concatenate([a["ffn_ew1"], a["ffn_ew2"]], axis=2))
    shared_up = _np.concatenate([up(halves(a["ffn_sw1"])), up(halves(a["ffn_sw2"]))], axis=2)
    w_up = _np.concatenate([experts_up, shared_up])
    w_down = _np.concatenate([a["ffn_ew3"], a["ffn_sw3"].reshape(2, INTER, DIM)])
    b1 = _np.concatenate([a["ffn_eb1"], a["ffn_sb1"].reshape(2, INTER)])
    b2 = _np.concatenate([a["ffn_eb2"], a["ffn_sb2"].reshape(2, INTER)])
    w_ffn = _np.concatenate([w_up, w_down, b1[:, :, None], b2[:, :, None]], axis=2)
    b12 = _np.concatenate([a["ffn_eb1"], a["ffn_eb2"]], axis=1)
    b3 = _np.concatenate([a["ffn_eb3"], a["ffn_sb3"][None]])
    router = a["ffn_router_w"].reshape(KT, P, EXPERTS).transpose(1, 0, 2)
    rows = _np.stack([a["ffn_router_b"], a["ffn_router_bias"], _np.arange(EXPERTS, dtype=_np.float32) - 64.0])
    w_o = a["attn_Wo"].reshape(DIM, KV, QPK, HD).transpose(1, 3, 2, 0).reshape(KV, P, W_O)
    w_attn = _np.concatenate([heads(a["attn_Wk"], KV), heads(a["attn_Wq"], HEADS), heads(a["attn_Wv"], KV), w_o], axis=2)

    inv_freq = (1.0 / _np.float32(10000.0) ** (_np.arange(0, HD, 2, dtype=_np.float32) / _np.float32(HD))).astype(_np.float32)
    freqs = _np.arange(SEQ, dtype=_np.float32)[None, :] * inv_freq[:, None]
    cos = _np.cos(_np.concatenate([freqs, freqs])).astype(_np.float32)
    sin = _np.concatenate([-_np.sin(freqs), _np.sin(freqs)]).astype(_np.float32)
    q, k = _np.arange(P)[:, None], _np.arange(P)[None, :]
    mask = _np.concatenate([_np.where(k >= q, 0.0, -BIG), _np.where(k <= q, 0.0, -BIG)], axis=1).astype(_np.float32)
    tri = _np.triu(_np.ones((P, P), _np.float32), 1)
    tile_index = _np.tile(_np.arange(SLOT_TILES, dtype=_np.float32), (P, 1))
    consts = _np.concatenate([_np.eye(P, dtype=_np.float32), cos, sin, mask, tri, tile_index], axis=1)

    arrays = {"x": a["attn_hidden_states"].reshape(TOKENS, DIM), "w_ffn": w_ffn, "b12": b12, "b3": b3, "router": router,
              "rows": rows, "w_attn": w_attn, "consts": consts}
    nc = _bacc.Bacc("TRN2", target_bir_lowering=False, num_devices=1)
    args = []
    for name in arrays:
        arrays[name] = _np.ascontiguousarray(arrays[name])
        args.append(nc.dram_tensor(name, arrays[name].shape, _mybir.dt.from_np(arrays[name].dtype), kind="ExternalInput").ap())
    args.append(nc.dram_tensor("out", (TOKENS, DIM), _mybir.dt.float32, kind="ExternalOutput").ap())
    macaron_block(nc, *args)
    r = _run(nc, [arrays], core_ids=[0])
    return r.results[0]["out"].reshape(BATCH, SEQ, DIM)
```

```python
from contextlib import ExitStack

import concourse.bass as bass
from concourse import mybir

F32 = mybir.dt.float32
F32R = mybir.dt.float32r
ACT = mybir.ActivationFunctionType
ALU = mybir.AluOpType
AX_X = mybir.AxisListType.X

P = 128
BATCH, SEQ, DIM = 8, 256, 512
TOKENS = BATCH * SEQ
TILES = TOKENS // P
KT = DIM // P
CHUNK = 512
CHUNKS = TOKENS // CHUNK
CT = CHUNK // P

EXPERTS, INTER, GROUPS_R = 16, 128, 4
SLICES = EXPERTS + 2
W_UP, W_DOWN = KT * INTER, DIM
W_SLICE = 2 * W_UP + W_DOWN
RAW_SLICE = W_SLICE + 2
SHARED = 2 * RAW_SLICE + DIM

HEADS, KV, HD = 32, 8, 128
QPK = HEADS // KV
PROJ = QPK + 2
W_QKV = PROJ * DIM
W_O = QPK * DIM
EPS = 1e-5
RING = 4
OWNERS = RING + 1
SLOT_TILES = -(-(2 * TILES + EXPERTS - 1) // RING) * RING
TRI_AT = 3 * P + 2 * SEQ
BIG = 1e30
PARTS = ((0, 0), (0, 1), (1, 0))


def bc(ap, shape):
    return ap.unsqueeze(len(shape) - 1).to_broadcast(list(shape))


def columns(XT, at, width):
    if len(XT.shape) == 3:
        return XT[:, :, bass.ds(at, width)]
    half = TOKENS // 2
    return XT[:, at // half, :, at % half:at % half + width]


class Semaphores:

    def __init__(self, nc, ctx, tag):
        self.nc, self.ctx, self.tag, self.all = nc, ctx, tag, []

    def __call__(self, name):
        self.all.append(self.ctx.enter_context(self.nc.semaphore(name + self.tag)))
        return self.all[-1]

    def clear(self, pool):
        for s in self.all:
            pool.sem_clear(s)


def each(eng, count, body):
    body(0)
    with eng.Fori(1, count) as i:
        body(i)


def normalise(nc, ctx, sem, tag, X, XT, ident, work, stats, moments, start, router_w=None, logits=None,
              router_in=None, x_in=None, ident_in=None, zeros=None, beside=None):
    mean_var, rstd = moments
    xn, rows = work
    split = len(XT) == 2
    std = ctx.enter_context(nc.sbuf_tensor(f"std{tag}", [P, TILES], F32))
    eps = ctx.enter_context(nc.sbuf_tensor(f"eps{tag}", [P, 1], F32))

    stats_done, aggr_done, std_done, rstd_done = sem("stats_done"), sem("aggr_done"), sem("std_done"), sem("rstd_done")
    xn_ready, turned, high_ready, low_ready, eps_set = (
        sem("xn_ready"), sem("turned"), sem("high_ready"), sem("low_ready"), sem("eps_set"))

    rows_done, rows_copied = sem("rows_done"), sem("rows_copied")

    with ExitStack() as inner:
        bank = [inner.enter_context(nc.psum_tensor(f"turn{i}{tag}", [P, KT, P], F32)) for i in range(CT)]
        if router_w is not None:
            logit_rows = [inner.enter_context(nc.psum_tensor(f"logit_rows{i}{tag}", [P, CHUNK], F32)) for i in range(2)]
        block = inner.enter_context(nc.Block())

        def is_first(c):
            return isinstance(c, int) and c == 0

        @block.vector
        def _(dve):
            dve.memset(eps[:], EPS).then_inc(eps_set, 1)
            if x_in is not None:
                for t in range(TILES):
                    if t % CT == 0:
                        dve.wait_ge(x_in[t // CT], 16)
                    dve.bn_stats(stats[:, t, :], X[:, t, :]).then_inc(stats_done, 1)
                dve.wait_ge(stats_done, TILES)
            for t in range(TILES):
                dve.bn_aggr(mean_var[:, t, :], stats[:, t, :]).then_inc(aggr_done, 1)
            dve.wait_ge(std_done, 1)
            dve.reciprocal(rstd[:], std[:]).then_inc(rstd_done, 1)
            dve.wait_ge(rstd_done, 1)

            def low_parts(c):
                for b in range(CT):
                    cols = bass.ds((c * CT + b) * P, P)
                    dve.wait_ge(high_ready, c * CT + b + 1)
                    dve.tensor_tensor(XT[1][:, :, cols], bank[b][:], XT[0][:, :, cols].bitcast(F32),
                                      ALU.subtract).then_inc(low_ready, 1)

            def four_tiles(c):
                for b in range(CT):
                    t = c * CT + b
                    if not is_first(c):
                        dve.wait_ge(turned, t - CT + 1)
                    dve.tensor_scalar(xn[:, b, :], X[:, t, :], mean_var[:, t, 0:1], rstd[:, bass.ds(t, 1)],
                                      ALU.subtract, ALU.mult).then_inc(xn_ready, 1)
                if split and not is_first(c):
                    low_parts(c - 1)
            each(dve, CHUNKS, four_tiles)
            if split:
                low_parts(CHUNKS - 1)

        if zeros is not None:
            @block.gpsimd
            def _(pool):
                pool.memset(zeros[0][:], 0.0).then_inc(zeros[1], 1)
        elif beside:
            @block.gpsimd
            def _(pool):
                for i in range(beside[2]):
                    beside[1](pool, i)

        @block.scalar
        def _(act):
            act.wait_ge(eps_set, 1)
            act.wait_ge(aggr_done, TILES)
            act.activation(std[:], mean_var[:, :, 1], ACT.Sqrt, bias=eps[:, 0:1]).then_inc(std_done, 1)

            def copy_rows(c, half):
                act.wait_ge(rows_done, c + 1)
                act.activation(rows[0:EXPERTS, bass.ds(c * CHUNK, CHUNK)], logit_rows[half][0:EXPERTS, :], ACT.Copy).then_inc(rows_copied, 1)

            def four_tiles(c):
                for b in range(CT):
                    t = c * CT + b
                    act.wait_ge(turned, t + 1)
                    act.activation(columns(XT[0], t * P, P), bank[b][:], ACT.Copy).then_inc(high_ready, 1)

            for c in range(CHUNKS):
                four_tiles(c)
                if router_w is not None and c:
                    copy_rows(c - 1, (c - 1) % 2)
                if beside and c < CHUNKS - 1:
                    for i in range(c * beside[2] // (CHUNKS - 1), (c + 1) * beside[2] // (CHUNKS - 1)):
                        beside[0](act, i)
            if router_w is not None:
                copy_rows(CHUNKS - 1, 1)

        if start:
            block.sync(start)

        @block.tensor
        def _(pe):
            def route(c, half):
                pe.wait_ge(high_ready, (c + 1) * CT)
                if c >= 2:
                    pe.wait_ge(rows_copied, c - 1)
                for k in range(KT):
                    last = pe.matmul(logit_rows[half][0:EXPERTS, :], router_w[:, k, :], columns(XT[0], c * CHUNK, CHUNK)[:, k, :],
                                     start=(k == 0), stop=(k == KT - 1))
                last.then_inc(rows_done, 1)

            def four_tiles(c):
                for b in range(CT):
                    t = c * CT + b
                    pe.wait_ge(xn_ready, t + 1)
                    if not is_first(c):
                        pe.wait_ge(low_ready if split else high_ready, t - CT + 1)
                    for k in range(KT):
                        last = pe.transpose(bank[b][:, k, :], xn[:, b, k * P:(k + 1) * P], ident[:])
                    last.then_inc(turned, 1)

            if ident_in is not None:
                pe.wait_ge(ident_in, 16)
            if router_w is None:
                each(pe, CHUNKS, four_tiles)
            else:
                for c in range(CHUNKS):
                    four_tiles(c)
                    if c:
                        if c == 1:
                            pe.wait_ge(router_in, 16)
                        route(c - 1, (c - 1) % 2)
                route(CHUNKS - 1, 1)
                pe.wait_ge(rows_copied, CHUNKS)
                for t in range(TILES):
                    pe.transpose(logits[:, t * EXPERTS:(t + 1) * EXPERTS], rows[0:EXPERTS, t * P:(t + 1) * P],
                                 ident[0:EXPERTS, 0:EXPERTS])


def shared_expert(nc, ctx, inner, sem, tag, first_chunk, X, XT, picks, ident, weights, split=False):
    w, b, b3, w_in = weights

    def bank(name):
        return inner.enter_context(nc.psum_tensor(name + tag, [P, CHUNK], F32))

    up1, up2, y = [bank(f"up1_{j}_{first_chunk}") for j in range(2)], bank(f"up2_{first_chunk}"), [bank(f"y{t}_{first_chunk}") for t in range(CT)]
    gates, silu, prod = (ctx.enter_context(nc.sbuf_tensor(f"{x}_{first_chunk}{tag}", [P, 2, CHUNK], F32)) for x in ("gates", "silu", "prod"))
    gates_ones, gates_turned, gates_copied, up1_done, up2_done, silu_done, lin_done, prod_done, y_done, y_added = (
        sem(f"{x}_{first_chunk}") for x in
        "gates_ones gates_turned gates_copied up1_done up2_done silu_done lin_done prod_done y_done y_added".split())

    products_of = PARTS if split else ((0, 0),)
    if split:
        def parts(name, shape):
            return [ctx.enter_context(nc.sbuf_tensor(f"{name}_{x}{tag}", shape, F32R)) for x in ("high", "low")]
        w_parts, x_parts, p_parts = parts("s_w", [P, 2, W_SLICE]), parts("s_xt", [P, KT, 2 * CHUNK]), parts("s_prod", [P, 2, CHUNK])
        high_done, low_done, p_high, p_low = (sem(f"s_{x}") for x in "high_done low_done p_high p_low".split())

        def w_piece(j, at, width):
            return [t[:, j, at:at + width] for t in (w, *w_parts)]

        def x_piece(i, k):
            return [columns(XT, (first_chunk + i) * CHUNK, CHUNK)[:, k:k + 2, :]] + [t[:, k:k + 2, i * CHUNK:(i + 1) * CHUNK] for t in x_parts]
        pieces = [w_piece(0, 0, W_UP), x_piece(0, 0), x_piece(0, 2), w_piece(0, W_UP, W_UP), w_piece(1, 0, W_UP), w_piece(1, W_UP, W_UP),
                  w_piece(0, 2 * W_UP, W_DOWN), w_piece(1, 2 * W_UP, W_DOWN), x_piece(1, 0), x_piece(1, 2)]

        def piece_high(act, m):
            act.wait_ge(w_in, 48)
            act.activation(pieces[m][1], pieces[m][0], ACT.Copy).then_inc(high_done, 1)

        def piece_low(dve, m):
            dve.wait_ge(high_done, m + 1)
            dve.tensor_tensor(pieces[m][2], pieces[m][0], pieces[m][1].bitcast(F32), ALU.subtract).then_inc(low_done, 1)

        def product_high(act, i, j):
            act.wait_ge(prod_done, 2 * i + j + 1)
            if i:
                act.wait_ge(y_done, i * CT)
            act.activation(p_parts[0][:, j, :], prod[:, j, :], ACT.Copy).then_inc(p_high, 1)

        def product_low(dve, i, j):
            dve.wait_ge(p_high, 2 * i + j + 1)
            dve.tensor_tensor(p_parts[1][:, j, :], prod[:, j, :], p_parts[0][:, j, :].bitcast(F32), ALU.subtract).then_inc(p_low, 1)

    def up(pe, i, j):
        s, at_token = 2 * i + j, (first_chunk + i) * CHUNK
        pe.wait_ge(w_in, 48)
        if i:
            pe.wait_ge(silu_done, s - 1)
        for out, at, done in ((up1[j], 0, up1_done), (up2, W_UP, up2_done)):
            if out is up2 and s:
                pe.wait_ge(lin_done, s)
            if split:
                pe.wait_ge(low_done, len(pieces) if i else {(0, 0): 3, (0, W_UP): 4, (1, 0): 5, (1, W_UP): 6}[(j, at)])
                tokens = [t[:, :, i * CHUNK:(i + 1) * CHUNK] for t in x_parts]
            else:
                tokens = [columns(XT, at_token, CHUNK)]
            for k in range(KT):
                for m, (u, v) in enumerate(products_of):
                    last = pe.matmul(out[:], (w_parts if split else [w])[u][:, j, at + k * P:at + (k + 1) * P], tokens[v][:, k, :],
                                     start=(k == 0 and m == 0), stop=(k == KT - 1 and m == len(products_of) - 1))
            last.then_inc(done, 1)

    def turn_gates(pe, i, out):
        if i:
            pe.wait_ge(gates_copied, i)
        for t in range(CT):
            last = pe.transpose(out[0:EXPERTS, t * P:(t + 1) * P], picks[:, (first_chunk + i) * CT + t, :], ident[:])
        last.then_inc(gates_turned, 1)

    def copy_gates(dve, i, turned):
        if i == 0:
            dve.memset(gates[0:EXPERTS + 1, :, :], 1.0).then_inc(gates_ones, 1)
            dve.wait_ge(gates_ones, 1)
        dve.wait_ge(gates_turned, i + 1)
        dve.tensor_copy(gates[0:EXPERTS, i, :], turned[0:EXPERTS, :]).then_inc(gates_copied, 1)

    def hidden(act, i, slices=range(2)):
        for j in slices:
            s = 2 * i + j
            act.wait_ge(up1_done, s + 1)
            if i:
                act.wait_ge(prod_done, s - 1)
            act.activation(silu[:, j, :], up1[j][:], ACT.Silu, bias=b[:, j, 0:1]).then_inc(silu_done, 1)
            act.wait_ge(up2_done, s + 1)
            if i:
                act.wait_ge(*((p_low, s - 1) if split else (y_done, i * CT)))
            act.activation(prod[:, j, :], up2[:], ACT.Identity, bias=b[:, j, 1:2]).then_inc(lin_done, 1)

    def products(pool, i, slices=range(2)):
        for j in slices:
            s = 2 * i + j
            pool.wait_ge(silu_done, s + 1)
            pool.wait_ge(lin_done, s + 1)
            pool.tensor_tensor(prod[:, j, :], silu[:, j, :], prod[:, j, :], ALU.mult).then_inc(prod_done, 1)

    def down(pe, i):
        if i:
            pe.wait_ge(y_added, i * CT)
        pe.wait_ge(gates_copied, i + 1)

        def bias(t):
            pe.matmul(y[t][:], gates[0:EXPERTS + 1, i, t * P:(t + 1) * P], b3[0:EXPERTS + 1, :], start=True, stop=False)

        def project(t, j):
            pe.wait_ge(p_low if split else prod_done, 2 * i + j + 1)
            for m, (u, v) in enumerate(products_of):
                last = pe.matmul(y[t][:], (p_parts if split else [prod])[u][:, j, t * P:(t + 1) * P],
                                 (w_parts if split else [w])[v][:, j, 2 * W_UP:W_SLICE],
                                 start=False, stop=(j == 1 and m == len(products_of) - 1))
            if j == 1:
                last.then_inc(y_done, 1)

        if split:
            pe.wait_ge(low_done, 8)
            for step in (bias, lambda t: project(t, 0), lambda t: project(t, 1)):
                for t in range(CT):
                    step(t)
        else:
            for t in range(CT):
                bias(t)
                project(t, 0)
                project(t, 1)

    def add(dve, i, then=lambda t: None):
        for t in range(CT):
            at = (first_chunk + i) * CT + t
            dve.wait_ge(y_done, i * CT + t + 1)
            dve.scalar_tensor_tensor(X[:, at, :], y[t][:], 0.5, X[:, at, :], ALU.mult, ALU.add).then_inc(y_added, 1)
            if t:
                then(at - 1)
        then(at)

    splits = (piece_high, piece_low, product_high, product_low) if split else None
    return up, turn_gates, copy_gates, hidden, products, down, add, y_added, splits, gates


def route_and_share(nc, ctx, sem, pool_sem, tag, X, XT, moments, logits, rows, tri, tile_index, ident, weights, routed, picks, xslots, filled,
                    late_experts, load_experts):
    mean_var, rstd = moments
    pos, half_gate, tile_expert, round_experts = routed
    n = TILES * EXPERTS
    G3 = (P, TILES, GROUPS_R)
    E3 = (P, TILES, EXPERTS)
    three = "p (t e) -> p t e"

    def sb(name, shape, dt=F32):
        return ctx.enter_context(nc.sbuf_tensor(name + tag, shape, dt))

    lg, ex, sc, cand, one2 = (sb(x, [P, TILES, EXPERTS]) for x in ("lg", "ex", "sc", "cand", "one2"))
    ms, one = ex, [lg, one2]
    chosen = sb("chosen", [P, TILES + 1, EXPERTS])
    gmax, gcand, keep1, keep2, gleft = (
        sb(x, [P, TILES, GROUPS_R]) for x in ("gmax", "gcand", "keep1", "keep2", "gleft"))
    pen = gcand
    m, total, inv, m1, low = (sb(x, [P, TILES]) for x in ("m", "total", "inv", "m1", "low"))
    whole, tiles_e, upto, base = (sb(x, [P, EXPERTS]) for x in ("whole", "tiles_e", "upto", "base"))
    whole_i = sb("whole_i", [P, EXPERTS], mybir.dt.int32)
    ones_row = sb("ones_row", [P, P])
    owner, packed = sb("owner", [P, 2 + SLOT_TILES]), sb("packed", [P, SLOT_TILES // RING])
    xn = sb("xn", [P, RING, DIM])

    step, shifted, exped, chosen_ready, ones_set, counted = (
        sem("step"), sem("shifted"), sem("exped"), sem("chosen_ready"), sem("ones_set"), sem("counted"))
    gates_ready = sem("gates_ready")
    routed_ready, xn_ready = sem("routed_ready"), sem("xn_again")
    sent = [pool_sem(f"sent{i}_") for i in range(RING)]

    with ExitStack() as inner:
        up, turn_gates, copy_gates, shared_hidden, products, down, add, _, _, gates = shared_expert(
            nc, ctx, inner, sem, tag, 0, X, XT, picks, ident, weights)
        before = gates[:].rearrange("p i n -> p (i n)")[:, 0:SLOT_TILES * EXPERTS].rearrange("p (s e) -> p s e", e=EXPERTS)
        block = inner.enter_context(nc.Block())

        @block.vector
        def _(dve):
            done = [0]

            def link(ins):
                done[0] += 1
                ins.then_inc(step, 1)
                dve.wait_ge(step, done[0])

            def first_max(values, marks, candidate, idx, shape):
                link(dve.tensor_reduce(m1[:], values, AX_X, ALU.max))
                link(dve.tensor_tensor(candidate, values, bc(m1[:], shape), ALU.is_equal))
                link(dve.tensor_tensor(candidate, candidate, idx, ALU.mult))
                link(dve.tensor_reduce(low[:], candidate, AX_X, ALU.min))
                link(dve.tensor_tensor(marks, candidate, bc(low[:], shape), ALU.is_equal))

            idx_e = rows[:, 2, 0:EXPERTS].unsqueeze(1).to_broadcast(list(E3))
            idx_g = rows[:, 2, 0:GROUPS_R].unsqueeze(1).to_broadcast(list(G3))
            dve.memset(ones_row[:], 1.0).then_inc(ones_set, 1)
            dve.memset(chosen[:, TILES, :], 0.0).then_inc(ones_set, 1)
            dve.memset(owner[:], 0.0).then_inc(ones_set, 1)
            link(dve.tensor_tensor(lg[:], logits[:, 0:n].rearrange(three, t=TILES), rows[:, 0, :].unsqueeze(1).to_broadcast(list(E3)), ALU.add))
            link(dve.tensor_reduce(m[:], lg[:], AX_X, ALU.max))
            dve.tensor_tensor(lg[:], lg[:], bc(m[:], E3), ALU.subtract).then_inc(shifted, 1)
            dve.wait_ge(exped, 1)
            link(dve.tensor_reduce(total[:], ex[:], AX_X, ALU.add))
            link(dve.reciprocal(inv[:], total[:]))
            link(dve.tensor_tensor(sc[:], ex[:], bc(inv[:], E3), ALU.mult))
            link(dve.tensor_tensor(sc[:], sc[:], rows[:, 1, :].unsqueeze(1).to_broadcast(list(E3)), ALU.add))
            by_group = "p t (g e) -> p t g e"
            link(dve.tensor_reduce(gmax[:], sc[:].rearrange(by_group, g=GROUPS_R), AX_X, ALU.max))
            first_max(gmax[:], keep1[:], gcand[:], idx_g, G3)
            link(dve.scalar_tensor_tensor(gleft[:], keep1[:], -2 * BIG, gmax[:], ALU.mult, ALU.add))
            first_max(gleft[:], keep2[:], gcand[:], idx_g, G3)
            link(dve.tensor_tensor(keep1[:], keep1[:], keep2[:], ALU.add))
            link(dve.tensor_scalar(pen[:], keep1[:], -1.0, BIG, ALU.add, ALU.mult))
            link(dve.tensor_tensor(ms[:].rearrange(by_group, g=GROUPS_R), sc[:].rearrange(by_group, g=GROUPS_R),
                                   bc(pen[:], (P, TILES, GROUPS_R, EXPERTS // GROUPS_R)), ALU.add))
            first_max(ms[:], one[0][:], cand[:], idx_e, E3)
            link(dve.scalar_tensor_tensor(ms[:], one[0][:], -2 * BIG, ms[:], ALU.mult, ALU.add))
            first_max(ms[:], one[1][:], cand[:], idx_e, E3)
            dve.tensor_tensor(chosen[:, 0:TILES, :], one[0][:], one[1][:], ALU.add).then_inc(chosen_ready, 1)
            dve.wait_ge(chosen_ready, 1)
            dve.tensor_tensor(picks[:], sc[:], chosen[:, 0:TILES, :], ALU.mult).then_inc(gates_ready, 1)
            for k in range(2):
                link(dve.tensor_tensor(cand[:], sc[:], one[k][:], ALU.mult))
                link(dve.tensor_reduce(total[:], cand[:], AX_X, ALU.add))
                link(dve.tensor_scalar(half_gate[:, k, :], total[:], 0.5, None, ALU.mult))
            def rows_again(tiles):
                for t in tiles:
                    if t >= RING:
                        dve.wait_ge(sent[t % RING], 32 * (t // RING))
                    dve.tensor_scalar(xn[:, t % RING, :], X[:, t, :], mean_var[:, t, 0:1], rstd[:, t:t + 1],
                                      ALU.subtract, ALU.mult).then_inc(xn_ready, 1)

            rows_again(range(0, RING))
            dve.wait_ge(counted, 1)
            link(dve.tensor_scalar(whole[:], logits[:, n:n + EXPERTS], 1.0 / P, (P - 1.0) / P - 0.5 + 0.5 / P, ALU.mult, ALU.add))
            link(dve.tensor_copy(whole_i[:], whole[:]))
            link(dve.tensor_copy(tiles_e[:], whole_i[:]))
            link(dve.tensor_tensor_scan(upto[:], ones_row[:, 0:EXPERTS], tiles_e[:], 0.0, ALU.mult, ALU.add))
            link(dve.tensor_tensor(base[:], upto[:], tiles_e[:], ALU.subtract))
            link(dve.tensor_scalar(base[:], base[:], float(P), None, ALU.mult))
            link(dve.tensor_tensor(ms[:], logits[:, 0:n].rearrange(three, t=TILES), base[:].unsqueeze(1).to_broadcast(list(E3)), ALU.add))
            for k in range(2):
                link(dve.tensor_tensor(cand[:], ms[:], one[k][:], ALU.mult))
                link(dve.tensor_reduce(total[:], cand[:], AX_X, ALU.add))
                dve.tensor_copy(pos[:, k, :], total[:]).then_inc(routed_ready, 1)
            link(dve.tensor_tensor(before, upto[:].unsqueeze(1).to_broadcast([P, SLOT_TILES, EXPERTS]),
                                   bc(tile_index[:], (P, SLOT_TILES, EXPERTS)), ALU.is_le))
            dve.wait_ge(ones_set, 3)
            link(dve.tensor_reduce(owner[:, 2:2 + SLOT_TILES], before, AX_X, ALU.add))
            link(dve.tensor_scalar(owner[:, 2:2 + SLOT_TILES], owner[:, 2:2 + SLOT_TILES], EXPERTS - 1.0, None, ALU.min))
            dve.tensor_copy(tile_expert[:], owner[:, 2:2 + SLOT_TILES]).then_inc(routed_ready, 1)
            rounds = SLOT_TILES // RING
            link(dve.tensor_copy(packed[:], owner[:, OWNERS - 1:OWNERS + SLOT_TILES - RING:RING]))
            for b in reversed(range(OWNERS - 1)):
                link(dve.scalar_tensor_tensor(packed[:], packed[:], float(EXPERTS), owner[:, b:b + SLOT_TILES - RING + 1:RING],
                                              ALU.mult, ALU.add))
            dve.tensor_copy(round_experts[:], packed[:]).then_inc(routed_ready, 1)
            copy_gates(dve, 0, logits)
            rows_again(range(RING, 2 * CT + 2))
            dve.wait_ge(xn_ready, 2 * CT)
            add(dve, 0)
            copy_gates(dve, 1, logits)
            rows_again(range(2 * CT + 2, 3 * CT))
            products(dve, 1, [0])
            rows_again(range(3 * CT, 3 * CT + 1))
            products(dve, 1, [1])
            rows_again(range(3 * CT + 1, 4 * CT))
            add(dve, 1)

        if late_experts:
            @block.sync
            def _(sp):
                for e in late_experts:
                    sp.wait_ge(xn_ready, min(TILES, RING + 1 + 2 * (e - late_experts[0])))
                    load_experts(sp, [e])

        @block.gpsimd
        def _(pool):
            def send(c):
                for t in range(c * CT, (c + 1) * CT):
                    pool.wait_ge(routed_ready, 2)
                    pool.wait_ge(xn_ready, t + 1)
                    for k in range(2):
                        pool.indirect_dma_start(xslots, bass.IndirectOffsetOnAxis(ap=pos[:, k, t:t + 1], axis=0),
                                                xn[:, t % RING, :], None).then_inc(sent[t % RING], 16)

            products(pool, 0)
            pool.wait_ge(filled, 32)
            send(0)
            send(1)
            send(2)
            send(3)
            for i in range(RING):
                pool.wait_ge(sent[i], 32 * (TILES // RING))

        @block.scalar
        def _(act):
            act.wait_ge(shifted, 1)
            act.activation(ex[:], lg[:], ACT.Exp).then_inc(exped, 1)
            shared_hidden(act, 0)
            shared_hidden(act, 1)

        @block.tensor
        def _(pe):
            up(pe, 0, 0)
            up(pe, 0, 1)
            pe.wait_ge(ones_set, 2)
            pe.wait_ge(chosen_ready, 1)
            pe.matmul(logits[:, 0:n + EXPERTS], tri[:], chosen[:].rearrange("p t e -> p (t e)"), start=True, stop=False)
            for t in range(TILES):
                last = pe.matmul(logits[:, (t + 1) * EXPERTS:n + EXPERTS].rearrange(three, e=EXPERTS), ones_row[:],
                                 chosen[:, t, :].unsqueeze(1).to_broadcast([P, TILES - t, EXPERTS]),
                                 start=False, stop=(t == TILES - 1))
            last.then_inc(counted, 1)
            up(pe, 1, 0)
            pe.wait_ge(gates_ready, 1)
            pe.wait_ge(routed_ready, 2)
            turn_gates(pe, 0, logits)
            down(pe, 0)
            turn_gates(pe, 1, logits)
            up(pe, 1, 1)
            down(pe, 1)


def run_experts(nc, ctx, sem, pool_sem, tag, ident, W, w_in, b12, b12_in, b12_dram, load_shared, tile_expert, round_experts, xslots, yslots):
    def sb(name, shape, dt=F32):
        return ctx.enter_context(nc.sbuf_tensor(name + tag, shape, dt))

    xg, xgt = sb("xg", [P, RING, DIM]), sb("xgt", [P, 2, KT, P])
    act_in, silu, h, ht, yo = sb("act_in", [P, 2, 2 * INTER]), sb("silu_e", [P, 2, INTER]), sb("h", [P, 2, INTER]), sb("ht", [P, 2, P]), sb("yo", [P, RING, DIM])
    x_in = [sem(f"slots_in{i}_") for i in range(RING)]
    y_out = [pool_sem(f"slots_out{i}_") for i in range(RING)]
    turned, xt_copied, upped, biased, silued, multiplied, h_turned, h_copied, downed, y_copied = (
        sem("e_" + x) for x in "turned xt_copied upped biased silued multiplied h_turned h_copied downed y_copied".split())

    with ExitStack() as inner:
        def bank(name, width):
            return [inner.enter_context(nc.psum_tensor(f"{name}{i}{tag}", [P, CHUNK], F32))[:, 0:width] for i in range(2)]
        xt_bank = [b.rearrange("p (k n) -> p k n", k=KT) for b in bank("xtb", DIM)]
        up_bank, ht_bank, y_bank = bank("upb", 2 * INTER), bank("htb", P), bank("yb", DIM)
        block = inner.enter_context(nc.Block())

        def rounds(eng, step):
            def body(i):
                for r in range(RING):
                    step(i * RING + r, r)
            each(eng, SLOT_TILES // RING, body)

        @block.sync
        def _(sp):
            def step(j, r):
                if not (isinstance(j, int) and j < RING):
                    sp.wait_ge(turned, j - RING + 1)
                sp.dma_start(xg[:, r, :], xslots[bass.ds(j * P, P), :]).then_inc(x_in[r], 16)
                if isinstance(j, int) and j == RING - 1:
                    sp.dma_start(b12[:], b12_dram.partition_broadcast(P)).then_inc(b12_in, 16)
                    load_shared(sp)
            rounds(sp, step)

        @block.gpsimd
        def _(pool):
            def step(j, r):
                pool.wait_ge(y_copied, j + 1)
                pool.dma_start(yslots[bass.ds(j * P, P), :], yo[:, r, :]).then_inc(y_out[r], 16)
            rounds(pool, step)
            for r in range(RING):
                pool.wait_ge(y_out[r], 16 * (SLOT_TILES // RING))

        @block.tensor
        def _(pe):
            def turn(j, r):
                pe.wait_ge(x_in[r], 16 * (j // RING + 1) if isinstance(j, int) else 16 * (j // RING) + 16)
                if not (isinstance(j, int) and j < 2):
                    pe.wait_ge(xt_copied, j - 1)
                for k in range(KT):
                    last = pe.transpose(xt_bank[r % 2][:, k, :], xg[:, r, k * P:(k + 1) * P], ident[:])
                last.then_inc(turned, 1)

            def owner_of(j):
                return pe.value_load(tile_expert[0:1, bass.ds(j, 1)], min_val=0, max_val=EXPERTS - 1)

            def up(j, b, e, ks):
                pe.wait_ge(xt_copied, j + 1)
                if not (isinstance(j, int) and j < 2):
                    pe.wait_ge(biased, j - 1)
                for k in ks:
                    last = pe.matmul(up_bank[b], xgt[:, b, k, :], W[:, e, 2 * k * INTER:2 * (k + 1) * INTER],
                                     start=(k == 0), stop=(k == KT - 1))
                if ks[-1] == KT - 1:
                    last.then_inc(upped, 1)

            def turn_hidden(j, b):
                pe.wait_ge(multiplied, j + 1)
                if not (isinstance(j, int) and j < 2):
                    pe.wait_ge(h_copied, j - 1)
                pe.transpose(ht_bank[b], h[:, b, :], ident[:]).then_inc(h_turned, 1)

            def down(j, b, e):
                pe.wait_ge(h_copied, j + 1)
                if not (isinstance(j, int) and j < 2):
                    pe.wait_ge(y_copied, j - 1)
                pe.matmul(y_bank[b], ht[:, b, :], W[:, e, 2 * W_UP:W_SLICE], start=True, stop=True).then_inc(downed, 1)

            first, second = range(KT // 2), range(KT // 2, KT)

            def body(i):
                back = 0 if isinstance(i, int) else -2
                word = pe.value_load(round_experts[0:1, bass.ds(i, 1)], min_val=0, max_val=EXPERTS ** OWNERS - 1)
                owner = {b: word // EXPERTS ** (b + 2) % EXPERTS for b in range(back, OWNERS - 2)}
                for r in range(RING):
                    j = i * RING + r
                    turn(j, r)
                    if r - 1 >= back:
                        up(j - 1, (r + 1) % 2, owner[r - 1], first)
                    if r - 2 >= back:
                        turn_hidden(j - 2, r % 2)
                    if r - 1 >= back:
                        up(j - 1, (r + 1) % 2, owner[r - 1], second)
                    if r - 2 >= back:
                        down(j - 2, r % 2, owner[r - 2])
            pe.wait_ge(w_in, 16 * EXPERTS)
            each(pe, SLOT_TILES // RING, body)
            e1, e2 = owner_of(SLOT_TILES - 1), owner_of(SLOT_TILES - 2)
            up(SLOT_TILES - 1, 1, e1, first)
            turn_hidden(SLOT_TILES - 2, 0)
            up(SLOT_TILES - 1, 1, e1, second)
            down(SLOT_TILES - 2, 0, e2)
            turn_hidden(SLOT_TILES - 1, 1)
            down(SLOT_TILES - 1, 1, e1)

        @block.scalar
        def _(act):
            def silu_of(j, b):
                act.wait_ge(biased, j + 1)
                if not (isinstance(j, int) and j < 2):
                    act.wait_ge(multiplied, j - 1)
                act.activation(silu[:, b, :], act_in[:, b, 0:INTER], ACT.Silu).then_inc(silued, 1)

            def copy_out(j, r):
                act.wait_ge(downed, j + 1)
                if not (isinstance(j, int) and j < RING):
                    act.wait_ge(y_out[r], 16 * (j // RING))
                act.activation(yo[:, r, :], y_bank[r % 2], ACT.Copy).then_inc(y_copied, 1)

            def step(j, r):
                act.wait_ge(turned, j + 1)
                if not (isinstance(j, int) and j < 2):
                    act.wait_ge(upped, j - 1)
                act.activation(xgt[:, r % 2, :, :], xt_bank[r % 2], ACT.Copy).then_inc(xt_copied, 1)
                if not (isinstance(j, int) and j < 1):
                    silu_of(j - 1, (r + 1) % 2)
                if not (isinstance(j, int) and j < 2):
                    copy_out(j - 2, (r - 2) % RING)
            rounds(act, step)
            silu_of(SLOT_TILES - 1, 1)
            copy_out(SLOT_TILES - 2, RING - 2)
            copy_out(SLOT_TILES - 1, RING - 1)

        @block.vector
        def _(dve):
            def hidden(j, b):
                e = dve.value_load(tile_expert[0:1, bass.ds(j, 1)], min_val=0, max_val=EXPERTS - 1)
                dve.wait_ge(upped, j + 1)
                if not (isinstance(j, int) and j < 2):
                    dve.wait_ge(multiplied, j - 1)
                dve.tensor_tensor(act_in[:, b, :], up_bank[b], b12[:, e, :], ALU.add).then_inc(biased, 1)
                dve.wait_ge(silued, j + 1)
                dve.wait_ge(biased, j + 1)
                if not (isinstance(j, int) and j < 2):
                    dve.wait_ge(h_turned, j - 1)
                dve.tensor_tensor(h[:, b, :], silu[:, b, :], act_in[:, b, INTER:2 * INTER], ALU.mult).then_inc(multiplied, 1)

            def copy_turned(j, b):
                dve.wait_ge(h_turned, j + 1)
                if not (isinstance(j, int) and j < 2):
                    dve.wait_ge(downed, j - 1)
                dve.tensor_copy(ht[:, b, :], ht_bank[b]).then_inc(h_copied, 1)

            def step(j, r):
                if not (isinstance(j, int) and j < 2):
                    copy_turned(j - 2, r % 2)
                if not (isinstance(j, int) and j < 1):
                    hidden(j - 1, (r + 1) % 2)
            dve.wait_ge(b12_in, 16)
            rounds(dve, step)
            copy_turned(SLOT_TILES - 2, 0)
            hidden(SLOT_TILES - 1, 1)
            copy_turned(SLOT_TILES - 1, 1)


def combine(nc, ctx, sem, pool_sem, tag, X, XT, picks, ident, weights, pos, half_gate, yslots, stats, out_dram):
    ring = 2 * RING
    got = ctx.enter_context(nc.sbuf_tensor("got" + tag, [P, ring, 2, DIM], F32))
    landed = [pool_sem(f"landed{i}_") for i in range(ring)]
    first_added, added, stored, stats_ready = sem("first_added"), sem("both_added"), sem("stored"), sem("stats_ready")
    with ExitStack() as inner:
        turned = inner.enter_context(nc.psum_tensor("turned" + tag, [P, CHUNK], F32))
        up, turn_gates, copy_gates, shared_hidden, products, down, add_shared, y_added, splits, _ = shared_expert(
            nc, ctx, inner, sem, tag, 2, X, XT, picks, ident, weights, split=True)
        piece_high, piece_low, product_high, product_low = splits
        block = inner.enter_context(nc.Block())

        @block.gpsimd
        def _(pool):
            def fetch(first, end):
                for t in range(first, end):
                    if t >= ring:
                        pool.wait_ge(added, t - ring + 1)
                    for k in range(2):
                        pool.indirect_dma_start(got[:, t % ring, k, :], None, yslots,
                                                bass.IndirectOffsetOnAxis(ap=pos[:, k, t:t + 1], axis=0)).then_inc(landed[t % ring], 16)
            fetch(0, 5)
            products(pool, 0, [0])
            fetch(5, 7)
            products(pool, 0, [1])
            fetch(7, 9)
            products(pool, 1, [0])
            fetch(9, 15)
            products(pool, 1, [1])
            fetch(15, TILES)

        @block.scalar
        def _(act):
            for m in range(10):
                piece_high(act, m)
            shared_hidden(act, 0, [0])
            product_high(act, 0, 0)
            shared_hidden(act, 0, [1])
            product_high(act, 0, 1)
            shared_hidden(act, 1, [0])
            product_high(act, 1, 0)
            shared_hidden(act, 1, [1])
            product_high(act, 1, 1)

        @block.tensor
        def _(pe):
            turn_gates(pe, 0, turned)
            up(pe, 0, 0)
            turn_gates(pe, 1, turned)
            up(pe, 0, 1)
            up(pe, 1, 0)
            down(pe, 0)
            up(pe, 1, 1)
            down(pe, 1)

        @block.vector
        def _(dve):
            def add(t, k, done):
                dve.scalar_tensor_tensor(X[:, t, :], got[:, t % ring, k, :], half_gate[:, k, t:t + 1], X[:, t, :],
                                         ALU.mult, ALU.add).then_inc(done, 1)

            def add_experts(first, end, stats_behind=None):
                for t in range(first, end):
                    dve.wait_ge(landed[t % ring], 32 * (t // ring + 1))
                    add(t, 0, first_added)
                    dve.wait_ge(first_added, t + 1)
                    add(t, 1, added)
                    if stats_behind:
                        statistics(t - stats_behind)

            def statistics(t):
                if out_dram is None:
                    dve.wait_ge(added, t + 1)
                    if t >= 2 * CT:
                        dve.wait_ge(y_added, t - 2 * CT + 1)
                    dve.bn_stats(stats[:, t, :], X[:, t, :]).then_inc(stats_ready, 1)

            for m in range(5):
                piece_low(dve, m)
            copy_gates(dve, 0, turned)
            for m in range(5, 10):
                piece_low(dve, m)
            copy_gates(dve, 1, turned)
            add_experts(0, 2)
            product_low(dve, 0, 0)
            add_experts(2, 5)
            product_low(dve, 0, 1)
            add_experts(5, 3 * CT, stats_behind=5)
            dve.wait_ge(added, 3 * CT)
            add_shared(dve, 0)
            product_low(dve, 1, 0)
            add_experts(3 * CT, 3 * CT + 2)
            product_low(dve, 1, 1)
            add_experts(3 * CT + 2, TILES)
            for t in range(7, 3 * CT):
                statistics(t)
            dve.wait_ge(added, TILES)
            add_shared(dve, 1, statistics)

        if out_dram is not None:
            @block.sync
            def _(sp):
                for t in range(TILES):
                    sp.wait_ge(added, t + 1)
                    if t >= 2 * CT:
                        sp.wait_ge(y_added, t - 2 * CT + 1)
                    sp.dma_start(out_dram[:, t, :], X[:, t, :]).then_inc(stored, 16)
                sp.wait_ge(stored, 16 * TILES)


def split_steps(raw, Wqkv, raw_in, high_done, low_done):
    def piece_high(act, g, i):
        act.wait_ge(raw_in, 16 * (g + 1))
        cols = slice(i * DIM, (i + 1) * DIM)
        act.activation(Wqkv[0][:, cols], raw[:, cols], ACT.Copy).then_inc(high_done, 1)

    def piece_low(pool, g, i):
        pool.wait_ge(high_done, PROJ * g + i + 1)
        cols = slice(i * DIM, (i + 1) * DIM)
        pool.tensor_tensor(Wqkv[1][:, cols], raw[:, cols], Wqkv[0][:, cols].bitcast(F32), ALU.subtract).then_inc(low_done, 1)
    return piece_high, piece_low


def attention(nc, ctx, sem, X, XT, ident, stats, a_dram, loads, loaded, done_with):
    def sb(name, shape, dt=F32):
        return ctx.enter_context(nc.sbuf_tensor(name, shape, dt))

    Wo = [sb("wo_high", [P, W_O], F32R), sb("wo_low", [P, W_O], F32R)]
    swapped, straight = sb("swapped", [P, 2, CHUNK]), sb("straight", [P, 2, CHUNK])
    qk = sb("qk", [P, QPK + 1, CHUNK])
    v_turned = straight[:, 1, :]
    v = [sb("v_high", [P, CT, HD], F32R), sb("v_low", [P, CT, HD], F32R)]
    probs = sb("probs", [P, 2, QPK, P])
    probs_t = [sb("probs_t_high", [P, 2, QPK * P], F32R), sb("probs_t_low", [P, 2, QPK * P], F32R)]
    row_max, row_sum, row_inv = sb("row_max", [P, 2, QPK]), sb("row_sum", [P, 2, QPK]), sb("row_inv", [P, 2, QPK])
    heads_out = [sb("heads_high", [P, QPK, CHUNK], F32R), sb("heads_low", [P, QPK, CHUNK], F32R)]

    raw, rotary, masks, Wqkv = loads
    raw_qkv, raw_o = raw[:, 0:W_QKV], raw[:, 0:W_O]
    raw_qkv_in, raw_o_in, consts_in, qkv_high, qkv_low = loaded
    names = ("o_high o_low proj_done swap_done rope_mul rope_sin rope_add "
             "vt_copied v_turned_back v_copied v_split scored masked max_done sub_done exp_done sum_done inv_done p_ready "
             "p_turned pt_copied pt_split pv_done oh_done ol_done wo_done added").split()
    s = {name: sem("a_" + name) for name in names}
    (o_high, o_low, proj_done, swap_done, rope_mul, rope_sin, rope_add,
     vt_copied, v_back, v_copied, v_split, scored, masked, max_done, sub_done, exp_done, sum_done, inv_done, p_ready,
     p_turned, pt_copied, pt_split, pv_done, oh_done, ol_done, wo_done, added) = [s[x] for x in names]
    stats_ready = sem("a_stats_ready")
    ROPES = QPK + 1
    piece_high, piece_low = split_steps(raw, Wqkv, raw_qkv_in, qkv_high, qkv_low)
    NCH = KV * CHUNKS
    scale = float(HD) ** -0.5
    H = HD // 2

    with ExitStack() as inner:
        def bank(name, shape):
            return inner.enter_context(nc.psum_tensor(name, shape, F32))
        proj = [bank(f"proj{i}", [P, CHUNK]) for i in range(2)]
        score = [bank(f"score{i}", [P, QPK, P]) for i in range(2)]
        turn = bank("turn", [P, CT, P])
        pv = bank("pv", [P, QPK * P])
        yo = [bank(f"yo{i}", [P, DIM]) for i in range(2)]

        mix_bank = [pv, proj[1], pv, score[1].rearrange("p h q -> p (h q)")]
        turn_bank = [turn, proj[1].rearrange("p (h q) -> p h q", h=QPK), turn, score[0]]

        block = inner.enter_context(nc.Block())

        @block.sync
        def _(sp):
            sp.wait_ge(qkv_low, PROJ)
            sp.dma_start(raw_o, a_dram[0, :, W_QKV:W_QKV + W_O]).then_inc(raw_o_in, 16)
            with sp.Fori(1, KV) as g:
                sp.wait_ge(o_low, QPK * g)
                sp.dma_start(raw_qkv, a_dram[g, :, 0:W_QKV]).then_inc(raw_qkv_in, 16)
                sp.wait_ge(qkv_low, PROJ * g + PROJ)
                sp.dma_start(raw_o, a_dram[g, :, W_QKV:W_QKV + W_O]).then_inc(raw_o_in, 16)

        @block.tensor
        def _(pe):
            def project(n, g, c, i):
                pe.wait_ge(qkv_low, PROJ * g + i + 1)
                if i == 1:
                    if not (isinstance(n, int) and n == 0):
                        pe.wait_ge(ol_done, CT * n - 2)
                else:
                    pe.wait_ge(rope_mul, ROPES * n + max(i - 1, 0))
                for k in range(KT):
                    for m, (a, b) in enumerate(PARTS):
                        last = pe.matmul(proj[i % 2][:], Wqkv[a][:, i * DIM + k * P:i * DIM + (k + 1) * P],
                                         XT[b][:, k, bass.ds(c * CHUNK, CHUNK)],
                                         start=(k == 0 and m == 0), stop=(k == KT - 1 and m == 2))
                last.then_inc(proj_done, 1)

            def out_proj(n, g, t, heads=range(QPK)):
                if heads[0] == 0:
                    pe.wait_ge(o_low, QPK * g + QPK)
                    pe.wait_ge(ol_done, CT * n + t + 1)
                    pe.wait_ge(added, CT * n + max(t - 1, 0))
                for h in heads:
                    for m, (a, b) in enumerate(PARTS):
                        last = pe.matmul(yo[t % 2][:], heads_out[a][:, h, t * P:(t + 1) * P], Wo[b][:, h * DIM:(h + 1) * DIM],
                                         start=(h == 0 and m == 0), stop=(h == QPK - 1 and m == 2))
                if heads[-1] == QPK - 1:
                    last.then_inc(wo_done, 1)

            def turn_v(n):
                pe.wait_ge(vt_copied, n + 1)
                pe.wait_ge(pt_split, CT * n)
                for t in range(CT):
                    last = pe.transpose(turn[:, t, :], v_turned[:, t * P:(t + 1) * P], ident[:])
                last.then_inc(v_back, 1)

            def scores(n, u):
                pe.wait_ge(rope_add, ROPES * (n + 1))
                pe.wait_ge(masked, CT * n + max(u - 1, 0))
                if u == 1:
                    pe.wait_ge(ol_done, CT * n)
                key_tile = u ^ 1
                for h in range(QPK):
                    last = pe.matmul(score[u % 2][:, h, :], qk[:, 1 + h, u * P:(u + 1) * P],
                                     qk[:, 0, key_tile * P:(key_tile + 1) * P], start=True, stop=True)
                last.then_inc(scored, 1)

            def turn_probs(n, u):
                pe.wait_ge(p_ready, CT * n + u + 1)
                if u == 0:
                    pe.wait_ge(v_split, n + 1)
                elif u == 2:
                    pe.wait_ge(pt_split, CT * n + 1)
                elif u == 3:
                    pe.wait_ge(masked, CT * n + 3)
                for h in range(QPK):
                    last = pe.transpose(turn_bank[u][:, h, :], probs[:, u % 2, h, :], ident[:])
                last.then_inc(p_turned, 1)

            def mix(n, u):
                pe.wait_ge(pt_split, CT * n + u + 1)
                pe.wait_ge(ol_done, CT * n + (1 if u >= 2 else 0))
                if u == 3:
                    pe.wait_ge(masked, CT * n + 4)
                for m, (a, b) in enumerate(PARTS):
                    last = pe.matmul(mix_bank[u][:, :], v[a][:, u ^ 1, :], probs_t[b][:, u % 2, :], start=(m == 0), stop=(m == 2))
                last.then_inc(pv_done, 1)

            def chunk(n, g, c, before):
                project(n, g, c, 0)
                if before:
                    turn_probs(before[0], 3)
                    mix(before[0], 2)
                project(n, g, c, 1)
                if before:
                    mix(before[0], 3)
                for i in range(2, PROJ):
                    project(n, g, c, i)
                if before:
                    out_proj(*before, 0)
                turn_v(n)
                scores(n, 0)
                scores(n, 1)
                if before:
                    out_proj(*before, 1)
                scores(n, 2)
                scores(n, 3)
                if before:
                    out_proj(*before, 2, [0])
                turn_probs(n, 0)
                if before:
                    out_proj(*before, 2, [1, 2])
                turn_probs(n, 1)
                if before:
                    out_proj(*before, 2, [3])
                mix(n, 0)
                if before:
                    out_proj(*before, 3, [0, 1])
                mix(n, 1)
                if before:
                    out_proj(*before, 3, [2, 3])
                turn_probs(n, 2)

            chunk(0, 0, 0, None)
            chunk(1, 0, 1, (0, 0))
            with pe.Fori(1, NCH // 2) as pair:
                for n in (2 * pair, 2 * pair + 1):
                    chunk(n, n // CHUNKS, n % CHUNKS, (n - 1, (n - 1) // CHUNKS))
            turn_probs(NCH - 1, 3)
            mix(NCH - 1, 2)
            mix(NCH - 1, 3)
            for t in range(CT):
                out_proj(NCH - 1, KV - 1, t)

        def by_head(eng, body, split_qkv, split_o):
            def head(g, last):
                body(g * CHUNKS, lambda i: None)
                body(g * CHUNKS + 1, lambda i: split_o(g, i) if i < QPK else None)
                body(g * CHUNKS + 2, lambda i: None)
                body(g * CHUNKS + 3, lambda i: None if last else split_qkv(g + 1, i))

            each(eng, KV - 1, lambda g: head(g, False))
            head(KV - 1, True)

        @block.scalar
        def _(act):
            def split_qkv(g, i):
                act.wait_ge(proj_done, PROJ * CHUNKS * g - PROJ + i + 1)
                piece_high(act, g, i)

            def split_o(g, h):
                act.wait_ge(raw_o_in, 16 * (g + 1))
                act.wait_ge(wo_done, CHUNKS * CT * g)
                act.activation(Wo[0][:, h * DIM:(h + 1) * DIM], raw_o[:, h * DIM:(h + 1) * DIM], ACT.Copy).then_inc(o_high, 1)

            def exp(n, u):
                act.wait_ge(sub_done, CT * n + u + 1)
                act.activation(probs[:, u % 2, :, :], probs[:, u % 2, :, :], ACT.Exp, scale=scale).then_inc(exp_done, 1)

            def copy_turned(n, u):
                act.wait_ge(p_turned, CT * n + u + 1)
                act.wait_ge(pv_done, CT * n + max(u - 1, 0))
                act.activation(probs_t[0][:, u % 2, :], turn_bank[u].rearrange("p h q -> p (h q)"), ACT.Copy).then_inc(pt_copied, 1)

            def high(n, u):
                act.wait_ge(pv_done, CT * n + u + 1)
                act.activation(heads_out[0][:, :, u * P:(u + 1) * P], mix_bank[u].rearrange("p (h q) -> p h q", h=QPK), ACT.Copy).then_inc(oh_done, 1)

            def body(n, between):
                for r in range(ROPES):
                    act.wait_ge(proj_done, PROJ * n + r + 1)
                    act.wait_ge(rope_add, ROPES * n + max(r - 1, 0))
                    act.activation(swapped[0:H, r % 2, :], proj[r % 2][H:HD, :], ACT.Copy)
                    act.activation(swapped[H:HD, r % 2, :], proj[r % 2][0:H, :], ACT.Copy).then_inc(swap_done, 1)
                    if not (isinstance(n, int) and n == 0):
                        if r == 0:
                            copy_turned(n - 1, 3)
                            high(n - 1, 2)
                        elif r == 1:
                            high(n - 1, 3)
                    between(r)
                act.wait_ge(proj_done, PROJ * (n + 1))
                act.wait_ge(rope_add, ROPES * n + 4)
                act.activation(v_turned, proj[1][:], ACT.Copy).then_inc(vt_copied, 1)
                between(ROPES)
                act.wait_ge(v_back, n + 1)
                act.wait_ge(pv_done, CT * n)
                act.activation(v[0][:], turn[:], ACT.Copy).then_inc(v_copied, 1)
                exp(n, 0)
                exp(n, 1)
                copy_turned(n, 0)
                copy_turned(n, 1)
                exp(n, 2)
                high(n, 0)
                exp(n, 3)
                high(n, 1)
                copy_turned(n, 2)

            by_head(act, body, split_qkv, split_o)
            copy_turned(NCH - 1, 3)
            high(NCH - 1, 2)
            high(NCH - 1, 3)

        @block.gpsimd
        def _(pool):
            def split_qkv(g, i):
                piece_low(pool, g, i)

            def split_o(g, h):
                pool.wait_ge(o_high, QPK * g + h + 1)
                cols = slice(h * DIM, (h + 1) * DIM)
                pool.tensor_tensor(Wo[1][:, cols], raw_o[:, cols], Wo[0][:, cols].bitcast(F32), ALU.subtract).then_inc(o_low, 1)

            def body(n, between):
                for r in range(ROPES):
                    pool.wait_ge(swap_done, ROPES * n + r + 1)
                    part = swapped[:, r % 2, :].rearrange("p (b s) -> p b s", s=SEQ)
                    pool.tensor_tensor(part, part, rotary[:, 1, :].unsqueeze(1).to_broadcast([P, CHUNK // SEQ, SEQ]),
                                       ALU.mult).then_inc(rope_sin, 1)
                    between(r)
                between(ROPES)

                def subtract(u):
                    pool.wait_ge(max_done, CT * n + u + 1)
                    pool.tensor_tensor(probs[:, u % 2, :, :], probs[:, u % 2, :, :], bc(row_max[:, u % 2, :], (P, QPK, P)),
                                       ALU.subtract).then_inc(sub_done, 1)

                def divide(u):
                    pool.wait_ge(inv_done, CT * n + u + 1)
                    pool.tensor_tensor(probs[:, u % 2, :, :], probs[:, u % 2, :, :], bc(row_inv[:, u % 2, :], (P, QPK, P)),
                                       ALU.mult).then_inc(p_ready, 1)

                subtract(0)
                subtract(1)
                divide(0)
                divide(1)
                subtract(2)
                subtract(3)
                divide(2)
                divide(3)

            pool.wait_ge(consts_in, 32)
            by_head(pool, body, split_qkv, split_o)
            done_with.clear(pool)

        @block.vector
        def _(dve):
            def multiply(n, r):
                dve.wait_ge(swap_done, ROPES * n + r + 1)
                dve.wait_ge(rope_add, ROPES * n + max(r - 1, 0))
                if r == 1:
                    dve.wait_ge(v_back, n)
                dve.tensor_tensor(straight[:, r % 2, :].rearrange("p (b s) -> p b s", s=SEQ),
                                  proj[r % 2][:].rearrange("p (b s) -> p b s", s=SEQ),
                                  rotary[:, 0, :].unsqueeze(1).to_broadcast([P, CHUNK // SEQ, SEQ]), ALU.mult).then_inc(rope_mul, 1)

            def add_halves(n, r):
                dve.wait_ge(rope_sin, ROPES * n + r + 1)
                dve.wait_ge(rope_mul, ROPES * n + r + 1)
                dve.wait_ge(scored, CT * n)
                dve.tensor_tensor(qk[:, r, :], straight[:, r % 2, :], swapped[:, r % 2, :], ALU.add).then_inc(rope_add, 1)

            def mask_and_max(n, u):
                dve.wait_ge(scored, CT * n + u + 1)
                dve.wait_ge(p_turned, CT * n + max(u - 1, 0))
                dve.tensor_tensor(probs[:, u % 2, :, :], score[u % 2][:],
                                  masks[:, u % 2, :].unsqueeze(1).to_broadcast([P, QPK, P]), ALU.add).then_inc(masked, 1)
                dve.wait_ge(masked, CT * n + u + 1)
                dve.wait_ge(sub_done, CT * n + max(u - 1, 0))
                dve.tensor_reduce(row_max[:, u % 2, :], probs[:, u % 2, :, :], AX_X, ALU.max).then_inc(max_done, 1)

            def inverse_sum(n, u):
                dve.wait_ge(exp_done, CT * n + u + 1)
                dve.tensor_reduce(row_sum[:, u % 2, :], probs[:, u % 2, :, :], AX_X, ALU.add).then_inc(sum_done, 1)
                dve.wait_ge(sum_done, CT * n + u + 1)
                dve.wait_ge(p_ready, CT * n + max(u - 1, 0))
                dve.reciprocal(row_inv[:, u % 2, :], row_sum[:, u % 2, :]).then_inc(inv_done, 1)

            def low(n, u):
                dve.wait_ge(oh_done, CT * n + u + 1)
                dve.tensor_tensor(heads_out[1][:, :, u * P:(u + 1) * P], mix_bank[u].rearrange("p (h q) -> p h q", h=QPK),
                                  heads_out[0][:, :, u * P:(u + 1) * P].bitcast(F32), ALU.subtract).then_inc(ol_done, 1)

            def v_low(n):
                dve.wait_ge(v_copied, n + 1)
                dve.tensor_tensor(v[1][:], turn[:], v[0][:].bitcast(F32), ALU.subtract).then_inc(v_split, 1)

            def probs_low(n, u):
                dve.wait_ge(pt_copied, CT * n + u + 1)
                dve.tensor_tensor(probs_t[1][:, u % 2, :], turn_bank[u].rearrange("p h q -> p (h q)"),
                                  probs_t[0][:, u % 2, :].bitcast(F32), ALU.subtract).then_inc(pt_split, 1)

            def add_out(n, c, t):
                dve.wait_ge(wo_done, CT * n + t + 1)
                dve.tensor_tensor(X[:, c * CT + t, :], yo[t % 2][:], X[:, c * CT + t, :], ALU.add).then_inc(added, 1)

            def chunk(n, before):
                multiply(n, 0)
                if before:
                    probs_low(before[0], 3)
                    low(before[0], 2)
                for r in range(1, ROPES):
                    multiply(n, r)
                    add_halves(n, r - 1)
                    if r == 1 and before:
                        low(before[0], 3)
                add_halves(n, ROPES - 1)
                if before:
                    add_out(*before, 0)
                mask_and_max(n, 0)
                mask_and_max(n, 1)
                v_low(n)
                inverse_sum(n, 0)
                inverse_sum(n, 1)
                if before:
                    add_out(*before, 1)
                mask_and_max(n, 2)
                probs_low(n, 0)
                mask_and_max(n, 3)
                probs_low(n, 1)
                inverse_sum(n, 2)
                low(n, 0)
                inverse_sum(n, 3)
                if before:
                    add_out(*before, 2)
                low(n, 1)
                if before:
                    add_out(*before, 3)
                probs_low(n, 2)

            def statistics(n):
                for t in range(CT):
                    at = (n % CHUNKS) * CT + t
                    dve.wait_ge(added, CT * n + t + 1)
                    dve.bn_stats(stats[:, at, :], X[:, at, :]).then_inc(stats_ready, 1)

            dve.wait_ge(consts_in, 32)
            chunk(0, None)
            with dve.Fori(1, NCH - CHUNKS + 1) as n:
                chunk(n, (n - 1, (n - 1) % CHUNKS))
            for n in range(NCH - CHUNKS + 1, NCH):
                chunk(n, (n - 1, (n - 1) % CHUNKS))
                statistics(n - 1)
            probs_low(NCH - 1, 3)
            low(NCH - 1, 2)
            low(NCH - 1, 3)
            for t in range(CT):
                add_out(NCH - 1, CHUNKS - 1, t)
            statistics(NCH - 1)


def macaron_block(nc, x, w_ffn, b12_dram, b3_dram, router_dram, rows_dram, w_attn, consts_dram, out):
    x_v = x.rearrange("(t p) d -> p t d", p=P)
    out_v = out.rearrange("(t p) d -> p t d", p=P)
    xslots = nc.dram_tensor("xslots", [SLOT_TILES * P, DIM], F32, kind="Internal").ap()
    yslots = nc.dram_tensor("yslots", [SLOT_TILES * P, DIM], F32, kind="Internal").ap()

    with ExitStack() as ctx:
        def sb(name, shape, dt=F32):
            return ctx.enter_context(nc.sbuf_tensor(name, shape, dt))
        X = sb("X", [P, TILES, DIM])
        ident = sb("ident", [P, P])
        stats = sb("stats", [P, TILES, 6])
        filled = ctx.enter_context(nc.semaphore("filled"))
        x_in = [ctx.enter_context(nc.semaphore(f"x_in{c}")) for c in range(CHUNKS)]
        ident_in = ctx.enter_context(nc.semaphore("ident_in"))

        def ffn(tag, first, last, sem):
            with ExitStack() as own:
                pool_sem = Semaphores(nc, ctx, tag)

                def sb(name, shape, dt=F32, ctx=own):
                    return ctx.enter_context(nc.sbuf_tensor(name + tag, shape, dt))
                XT = sb("xt", [P, 2, KT, TOKENS // 2])
                picks = sb("picks", [P, TILES, EXPERTS])
                pos = sb("pos", [P, 2, TILES], mybir.dt.uint32)
                half_gate = sb("half_gate", [P, 2, TILES])
                tile_expert = sb("tile_expert", [P, SLOT_TILES], mybir.dt.int32)
                round_experts = sb("round_experts", [P, SLOT_TILES // RING], mybir.dt.int32)
                zeroed, router_in = sem("zeroed"), sem("router_in")
                params_in, shared_in, w_in, b12_in = sem("params_in"), [sem("shared_in0"), sem("shared_in1")], sem("w_in"), sem("b12_in")

                def shared_weights(which, at):
                    w = at[:, 0:2 * W_SLICE].rearrange("p (j b) -> p j b", j=2)
                    b = at[:, 2 * W_SLICE:2 * W_SLICE + 4].rearrange("p (j b) -> p j b", j=2)
                    b3 = at[:, 2 * W_SLICE + 4:SHARED]
                    arrived = shared_in[which]

                    def load(sp):
                        sp.dma_start(w[:], w_ffn[EXPERTS:SLICES, :, 0:W_SLICE].rearrange("j p b -> p j b")).then_inc(arrived, 16)
                        sp.dma_start(b[:], w_ffn[EXPERTS:SLICES, :, W_SLICE:RAW_SLICE].rearrange("j p b -> p j b")).then_inc(arrived, 16)
                        sp.dma_start(b3[0:EXPERTS + 1, :], b3_dram).then_inc(arrived, 16)
                    return (w, b, b3, arrived), load

                weights_again, load_again = shared_weights(1, XT[:, 0, :, :].rearrange("p k n -> p (k n)"))
                with ExitStack() as experts_scope:
                    W = sb("w_experts", [P, EXPERTS, W_SLICE], ctx=experts_scope)
                    with ExitStack() as early:
                        weights, load_shared = shared_weights(0, sb("shared", [P, SHARED], ctx=early))
                        tri = sb("tri", [P, P], ctx=early)
                        router_w, rows = sb("router_w", [P, KT, EXPERTS], ctx=early), sb("rows", [P, 3, EXPERTS], ctx=early)
                        tile_index = sb("tile_index", [P, SLOT_TILES], ctx=early)
                        moments = sb("mean_var", [P, TILES, 2], ctx=early), sb("rstd", [P, TILES], ctx=early)
                        zeros = sb("zeros", [P, DIM // 2], ctx=early) if first else None
                        logits = early.enter_context(nc.psum_tensor("logits" + tag, [P, CHUNK], F32))

                        early_experts = 10 if first else EXPERTS

                        def load_experts(sp, experts):
                            for e in experts:
                                sp.dma_start(W[:, e, :], w_ffn[e, :, 0:W_SLICE]).then_inc(w_in, 16)

                        def start(sp):
                            if first:
                                for c in range(CHUNKS):
                                    sp.dma_start(X[:, c * CT:(c + 1) * CT, :], x_v[:, c * CT:(c + 1) * CT, :]).then_inc(x_in[c], 16)
                                sp.dma_start(ident[:], consts_dram[:, 0:P]).then_inc(ident_in, 16)
                            sp.dma_start(router_w[:], router_dram).then_inc(router_in, 16)
                            sp.dma_start(rows[:], rows_dram.partition_broadcast(P)).then_inc(params_in, 16)
                            sp.dma_start(tri[:], consts_dram[:, TRI_AT:TRI_AT + P]).then_inc(params_in, 16)
                            sp.dma_start(tile_index[:], consts_dram[:, TRI_AT + P:TRI_AT + P + SLOT_TILES]).then_inc(params_in, 16)
                            load_shared(sp)
                            if first:
                                sp.wait_ge(zeroed, 1)
                                for half in range(2):
                                    sp.dma_start(xslots.rearrange("(j p) d -> p j d", p=P)[:, :, half * (DIM // 2):(half + 1) * (DIM // 2)],
                                                 zeros[:].unsqueeze(1).to_broadcast([P, SLOT_TILES, DIM // 2])).then_inc(filled, 16)
                            load_experts(sp, range(0, early_experts))
                            sp.wait_ge(params_in, 48)

                        with ExitStack() as turning:
                            work = sb("n_xn", [P, CT, DIM], ctx=turning), sb("n_rows", [P, TOKENS], ctx=turning)
                            normalise(nc, turning, sem, tag, X, [XT], ident, work, stats, moments, start, router_w, logits,
                                      router_in, x_in if first else None, ident_in if first else None, (zeros, zeroed) if first else None)
                        with ExitStack() as routing:
                            route_and_share(nc, routing, sem, pool_sem, tag, X, XT, moments, logits, rows, tri, tile_index, ident,
                                            weights, (pos, half_gate, tile_expert, round_experts), picks, xslots, filled,
                                            range(early_experts, EXPERTS), load_experts)
                    with ExitStack() as late:
                        b12 = sb("b12", [P, EXPERTS, 2 * INTER], ctx=late)
                        run_experts(nc, late, sem, pool_sem, tag, ident, W, w_in, b12, b12_in, b12_dram, load_again, tile_expert, round_experts, xslots, yslots)
                with ExitStack() as late:
                    combine(nc, late, sem, pool_sem, tag, X, XT, picks, ident, weights_again, pos, half_gate, yslots,
                            stats, out_v if last else None)

        first_sems = ctx.enter_context(ExitStack())
        of_first = Semaphores(nc, first_sems, "_f1")
        ffn("_f1", True, False, of_first)
        with ExitStack() as own:
            sem = Semaphores(nc, ctx, "_a")
            def sb(name, shape, dt=F32, ctx=own):
                return ctx.enter_context(nc.sbuf_tensor(name, shape, dt))
            XT = [sb("xt_high", [P, KT, TOKENS], F32R), sb("xt_low", [P, KT, TOKENS], F32R)]
            raw = sb("raw", [P, W_QKV])
            rotary, masks = sb("rotary", [P, 2, SEQ]), sb("masks", [P, 2, P])
            Wqkv = [sb("wqkv_high", [P, W_QKV], F32R), sb("wqkv_low", [P, W_QKV], F32R)]
            raw_qkv_in, raw_o_in, consts_in, qkv_high, qkv_low = (
                sem(x) for x in "raw_qkv_in raw_o_in consts_in qkv_high qkv_low".split())
            piece_high, piece_low = split_steps(raw, Wqkv, raw_qkv_in, qkv_high, qkv_low)

            def start(sp):
                halves = "p (a b) -> p a b"
                sp.dma_start(raw[:], w_attn[0, :, 0:W_QKV]).then_inc(raw_qkv_in, 16)
                sp.dma_start(rotary[:], consts_dram[:, P:P + 2 * SEQ].rearrange(halves, a=2)).then_inc(consts_in, 16)
                sp.dma_start(masks[:], consts_dram[:, P + 2 * SEQ:2 * SEQ + 3 * P].rearrange(halves, a=2)).then_inc(consts_in, 16)

            with ExitStack() as turning:
                xn = sb("a_xn", [P, CT, DIM], ctx=turning)
                moments = sb("a_mean_var", [P, TILES, 2], ctx=turning), sb("a_rstd", [P, TILES], ctx=turning)
                normalise(nc, turning, sem, "_a", X, XT, ident, (xn, None), stats, moments, start,
                          beside=(lambda act, i: piece_high(act, 0, i), lambda pool, i: piece_low(pool, 0, i), PROJ))
            attention(nc, own, sem, X, XT, ident, stats, w_attn, (raw, rotary, masks, Wqkv),
                      (raw_qkv_in, raw_o_in, consts_in, qkv_high, qkv_low),
                      of_first)
        first_sems.close()
        ffn("_f2", False, True, Semaphores(nc, ctx, "_f2"))


def kernel(**inputs):
    import numpy as _np
    import concourse.bacc as _bacc
    from concourse import mybir as _mybir
    from concourse.bass_utils import run_bass_kernel_spmd as _run

    a = {k.replace("L0_", ""): _np.asarray(v) for k, v in inputs.items()}

    def up(w):
        return w.reshape(len(w), KT, P, -1).transpose(0, 2, 1, 3).reshape(len(w), P, -1)

    def halves(w):
        return w.reshape(DIM, 2, INTER).transpose(1, 0, 2)

    def heads(w, n):
        return w.reshape(KV, n // KV, HD, KT, P).transpose(0, 4, 1, 3, 2).reshape(KV, P, -1)

    experts_up = up(_np.concatenate([a["ffn_ew1"], a["ffn_ew2"]], axis=2))
    shared_up = _np.concatenate([up(halves(a["ffn_sw1"])), up(halves(a["ffn_sw2"]))], axis=2)
    w_up = _np.concatenate([experts_up, shared_up])
    w_down = _np.concatenate([a["ffn_ew3"], a["ffn_sw3"].reshape(2, INTER, DIM)])
    b1 = _np.concatenate([a["ffn_eb1"], a["ffn_sb1"].reshape(2, INTER)])
    b2 = _np.concatenate([a["ffn_eb2"], a["ffn_sb2"].reshape(2, INTER)])
    w_ffn = _np.concatenate([w_up, w_down, b1[:, :, None], b2[:, :, None]], axis=2)
    b12 = _np.concatenate([a["ffn_eb1"], a["ffn_eb2"]], axis=1)
    b3 = _np.concatenate([a["ffn_eb3"], a["ffn_sb3"][None]])
    router = a["ffn_router_w"].reshape(KT, P, EXPERTS).transpose(1, 0, 2)
    rows = _np.stack([a["ffn_router_b"], a["ffn_router_bias"], _np.arange(EXPERTS, dtype=_np.float32) - 64.0])
    w_o = a["attn_Wo"].reshape(DIM, KV, QPK, HD).transpose(1, 3, 2, 0).reshape(KV, P, W_O)
    w_attn = _np.concatenate([heads(a["attn_Wk"], KV), heads(a["attn_Wq"], HEADS), heads(a["attn_Wv"], KV), w_o], axis=2)

    inv_freq = (1.0 / _np.float32(10000.0) ** (_np.arange(0, HD, 2, dtype=_np.float32) / _np.float32(HD))).astype(_np.float32)
    freqs = _np.arange(SEQ, dtype=_np.float32)[None, :] * inv_freq[:, None]
    cos = _np.cos(_np.concatenate([freqs, freqs])).astype(_np.float32)
    sin = _np.concatenate([-_np.sin(freqs), _np.sin(freqs)]).astype(_np.float32)
    q, k = _np.arange(P)[:, None], _np.arange(P)[None, :]
    mask = _np.concatenate([_np.where(k >= q, 0.0, -BIG), _np.where(k <= q, 0.0, -BIG)], axis=1).astype(_np.float32)
    tri = _np.triu(_np.ones((P, P), _np.float32), 1)
    tile_index = _np.tile(_np.arange(SLOT_TILES, dtype=_np.float32), (P, 1))
    consts = _np.concatenate([_np.eye(P, dtype=_np.float32), cos, sin, mask, tri, tile_index], axis=1)

    arrays = {"x": a["attn_hidden_states"].reshape(TOKENS, DIM), "w_ffn": w_ffn, "b12": b12, "b3": b3, "router": router,
              "rows": rows, "w_attn": w_attn, "consts": consts}
    nc = _bacc.Bacc("TRN2", target_bir_lowering=False, num_devices=1)
    args = []
    for name in arrays:
        arrays[name] = _np.ascontiguousarray(arrays[name])
        args.append(nc.dram_tensor(name, arrays[name].shape, _mybir.dt.from_np(arrays[name].dtype), kind="ExternalInput").ap())
    args.append(nc.dram_tensor("out", (TOKENS, DIM), _mybir.dt.float32, kind="ExternalOutput").ap())
    macaron_block(nc, *args)
    r = _run(nc, [arrays], core_ids=[0])
    return r.results[0]["out"].reshape(BATCH, SEQ, DIM)
```
